# Optimizing a Trainium2 kernel written in Bass

```python
import numpy as np
import jax
import jax.numpy as jnp

def _softmax(x, axis=-1):
    return jax.nn.softmax(x, axis=axis)

def _gelu(x):
    return jax.nn.gelu(x, approximate=True)

def _silu(x):
    return jax.nn.silu(x)

def _sigmoid(x):
    return jax.nn.sigmoid(x)

def _layernorm(x, axis=-1, eps=1e-05):
    m = jnp.mean(x, axis=axis, keepdims=True)
    v = jnp.var(x, axis=axis, keepdims=True)
    return (x - m) / jnp.sqrt(v + eps)

def _scatter_add(tgt, idx, src, axis=0):
    return tgt.at[idx].add(src)

def _segment_sum(src, seg, n):
    return jax.ops.segment_sum(src, seg, n)
kernel_name = 'mk_vit_tower_d1_tok_img512_r4_fe20cc'

def setup_inputs(seed: int=0):
    np.random.seed(seed)
    _w = jnp.asarray

    def _rec_inputs():
        import jax
        import jax.numpy as jnp
        _rk = jax.random.key(seed)
        x = -0.000477451 + 1.00034 * jax.random.normal(jax.random.fold_in(_rk, 1), (8, 32, 32, 29), jnp.float32)
        return x
    x = _rec_inputs()

    def _L0_tok_setup():
        import jax, jax.numpy as jnp
        import numpy as np
        import math
        H, W_DIM, D_MODEL, B = (32, 32, 128, 128)
        F_TOTAL = 29
        SEQ_LEN = H * W_DIM

        def make_pe(seq_len: int, d_model: int) -> jnp.ndarray:
            position = np.arange(seq_len, dtype=np.float32)[:, None]
            div_term = np.exp(np.arange(0, d_model, 2, dtype=np.float32) * (-math.log(10000.0) / d_model))
            pe = np.zeros((seq_len, d_model), dtype=np.float32)
            pe[:, 0::2] = np.sin(position * div_term)
            pe[:, 1::2] = np.cos(position * div_term)
            return jnp.asarray(pe)
        key = jax.random.key(seed)
        k1, k2 = jax.random.split(key)
        state_tensor = jax.random.normal(k1, (B, H, W_DIM, F_TOTAL), dtype=jnp.float32)
        W = jax.random.normal(k2, (F_TOTAL, D_MODEL), dtype=jnp.float32) * 0.05
        return {'state_tensor': state_tensor, 'W': W}
    _L0_tok_all = _L0_tok_setup()
    _L0_tok_in = {k: v for k, v in _L0_tok_all.items() if k in ('W',)}
    del _L0_tok_all

    def _L0_attn_setup():
        import math
        import jax, jax.numpy as jnp
        import numpy as np
        B, N_COLS, CHANNELS, NUM_HEADS = (128, 128, 128, 8)
        D_HEAD = CHANNELS // NUM_HEADS
        key = jax.random.key(seed)
        ks = jax.random.split(key, 9)
        s = 1.0 / math.sqrt(CHANNELS)
        x = jax.random.normal(ks[0], (B, N_COLS, CHANNELS), dtype=jnp.float32)
        Wq = jax.random.uniform(ks[1], (CHANNELS, CHANNELS), jnp.float32, -s, s)
        bq = jax.random.uniform(ks[2], (CHANNELS,), jnp.float32, -s, s)
        Wk = jax.random.uniform(ks[3], (CHANNELS, CHANNELS), jnp.float32, -s, s)
        bk = jax.random.uniform(ks[4], (CHANNELS,), jnp.float32, -s, s)
        Wv = jax.random.uniform(ks[5], (CHANNELS, CHANNELS), jnp.float32, -s, s)
        bv = jax.random.uniform(ks[6], (CHANNELS,), jnp.float32, -s, s)
        Wo = jax.random.uniform(ks[7], (CHANNELS, CHANNELS), jnp.float32, -s, s)
        bo = jax.random.uniform(ks[8], (CHANNELS,), jnp.float32, -s, s)
        return {'x': x, 'Wq': Wq, 'bq': bq, 'Wk': Wk, 'bk': bk, 'Wv': Wv, 'bv': bv, 'Wo': Wo, 'bo': bo}
    _L0_attn_all = _L0_attn_setup()
    _L0_attn_in = {k: v for k, v in _L0_attn_all.items() if k in ('Wq', 'bq', 'Wk', 'bk', 'Wv', 'bv', 'Wo', 'bo')}
    del _L0_attn_all

    def _L0_ffn_setup():
        import jax, jax.numpy as jnp
        import numpy as np
        B, T, C = (8, 256, 128)
        H = 256
        G, EG = (2, 4)
        E = G * EG
        K = 2
        LN_EPS = 1e-05

        def _swiglu(x):
            a, b = jnp.split(x, 2, axis=-1)
            return jax.nn.silu(a) * b
        key = jax.random.key(seed)
        ks = jax.random.split(key, 8)
        n = lambda k, shape, s: jax.random.normal(k, shape, dtype=jnp.float32) * s
        return {'x': n(ks[0], (B, T, C), 1.0), 'ln_scale': jnp.ones((C,), jnp.float32), 'ln_bias': jnp.zeros((C,), jnp.float32), 'shared_in_w': n(ks[1], (2 * H, C), 0.02), 'shared_out_w': n(ks[2], (C, H), 0.02), 'shared_out_b': jnp.zeros((C,), jnp.float32), 'expert_in_w': n(ks[3], (2 * H, C), 0.02), 'expert_out_weight': n(ks[4], (E, C, H), 0.02), 'expert_out_bias': jnp.zeros((E, C), jnp.float32), 'group_gate_w': n(ks[5], (G, C), 0.02), 'expert_gate_w': n(ks[6], (E, C), 0.02), 'group_bias': jnp.zeros((G,), jnp.float32), 'expert_bias': jnp.zeros((E,), jnp.float32)}
    _L0_ffn_all = _L0_ffn_setup()
    _L0_ffn_in = {k: v for k, v in _L0_ffn_all.items() if k in ('ln_scale', 'ln_bias', 'shared_in_w', 'shared_out_w', 'shared_out_b', 'expert_in_w', 'expert_out_weight', 'expert_out_bias', 'group_gate_w', 'expert_gate_w', 'group_bias', 'expert_bias')}
    del _L0_ffn_all
    return {'x': x, 'L0_tok_W': _L0_tok_in['W'], 'L0_attn_Wq': _L0_attn_in['Wq'], 'L0_attn_bq': _L0_attn_in['bq'], 'L0_attn_Wk': _L0_attn_in['Wk'], 'L0_attn_bk': _L0_attn_in['bk'], 'L0_attn_Wv': _L0_attn_in['Wv'], 'L0_attn_bv': _L0_attn_in['bv'], 'L0_attn_Wo': _L0_attn_in['Wo'], 'L0_attn_bo': _L0_attn_in['bo'], 'L0_ffn_ln_scale': _L0_ffn_in['ln_scale'], 'L0_ffn_ln_bias': _L0_ffn_in['ln_bias'], 'L0_ffn_shared_in_w': _L0_ffn_in['shared_in_w'], 'L0_ffn_shared_out_w': _L0_ffn_in['shared_out_w'], 'L0_ffn_shared_out_b': _L0_ffn_in['shared_out_b'], 'L0_ffn_expert_in_w': _L0_ffn_in['expert_in_w'], 'L0_ffn_expert_out_weight': _L0_ffn_in['expert_out_weight'], 'L0_ffn_expert_out_bias': _L0_ffn_in['expert_out_bias'], 'L0_ffn_group_gate_w': _L0_ffn_in['group_gate_w'], 'L0_ffn_expert_gate_w': _L0_ffn_in['expert_gate_w'], 'L0_ffn_group_bias': _L0_ffn_in['group_bias'], 'L0_ffn_expert_bias': _L0_ffn_in['expert_bias']}

def reference(x, L0_tok_W, L0_attn_Wq, L0_attn_bq, L0_attn_Wk, L0_attn_bk, L0_attn_Wv, L0_attn_bv, L0_attn_Wo, L0_attn_bo, L0_ffn_ln_scale, L0_ffn_ln_bias, L0_ffn_shared_in_w, L0_ffn_shared_out_w, L0_ffn_shared_out_b, L0_ffn_expert_in_w, L0_ffn_expert_out_weight, L0_ffn_expert_out_bias, L0_ffn_group_gate_w, L0_ffn_expert_gate_w, L0_ffn_group_bias, L0_ffn_expert_bias):
    import jax
    import jax.numpy as jnp

    def _L0_tok_ref(state_tensor, W):
        import jax, jax.numpy as jnp
        import numpy as np
        import math
        H, W_DIM, D_MODEL, B = (32, 32, 128, 128)
        F_TOTAL = 29
        SEQ_LEN = H * W_DIM

        def make_pe(seq_len: int, d_model: int) -> jnp.ndarray:
            position = np.arange(seq_len, dtype=np.float32)[:, None]
            div_term = np.exp(np.arange(0, d_model, 2, dtype=np.float32) * (-math.log(10000.0) / d_model))
            pe = np.zeros((seq_len, d_model), dtype=np.float32)
            pe[:, 0::2] = np.sin(position * div_term)
            pe[:, 1::2] = np.cos(position * div_term)
            return jnp.asarray(pe)
        b, h, w, f = state_tensor.shape
        s = h * w
        x = state_tensor.reshape(b, s, f)
        emb = jnp.einsum('bsf,fd->bsd', x, W)
        pe = make_pe(s * 2, W.shape[1])[:s]
        return emb + pe[None, :, :]

    def _L0_attn_ref(x, Wq, bq, Wk, bk, Wv, bv, Wo, bo):
        import math
        import jax, jax.numpy as jnp
        import numpy as np
        B, N_COLS, CHANNELS, NUM_HEADS = (128, 128, 128, 8)
        D_HEAD = CHANNELS // NUM_HEADS
        b, n, c = x.shape
        h, d = (NUM_HEADS, D_HEAD)

        def split_heads(t):
            return t.reshape(b, n, h, d).transpose(0, 2, 1, 3)
        Q = split_heads(x @ Wq + bq)
        K = split_heads(x @ Wk + bk)
        V = split_heads(x @ Wv + bv)
        scores = jnp.einsum('bhqd,bhkd->bhqk', Q, K)
        causal = jnp.tril(jnp.ones((n, n), dtype=jnp.float32))
        mask = (1.0 - causal) * -100000.0
        attn = jax.nn.softmax((scores + mask) / math.sqrt(d), axis=-1)
        out = jnp.einsum('bhqk,bhkd->bhqd', attn, V)
        out = out.transpose(0, 2, 1, 3).reshape(b, n, c)
        return out @ Wo + bo

    def _L0_ffn_ref(x, ln_scale, ln_bias, shared_in_w, shared_out_w, shared_out_b, expert_in_w, expert_out_weight, expert_out_bias, group_gate_w, expert_gate_w, group_bias, expert_bias):
        import jax, jax.numpy as jnp
        import numpy as np
        B, T, C = (8, 256, 128)
        H = 256
        G, EG = (2, 4)
        E = G * EG
        K = 2
        LN_EPS = 1e-05

        def _swiglu(x):
            a, b = jnp.split(x, 2, axis=-1)
            return jax.nn.silu(a) * b
        Bx, Tx, Cx = x.shape
        S = Bx * Tx
        flat = x.reshape(S, Cx)
        mu = flat.mean(-1, keepdims=True)
        var = ((flat - mu) ** 2).mean(-1, keepdims=True)
        flat = (flat - mu) * jax.lax.rsqrt(var + LN_EPS) * ln_scale + ln_bias
        h_shared = _swiglu(flat @ shared_in_w.T)
        out_shared = h_shared @ shared_out_w.T + shared_out_b
        g_logits = flat @ group_gate_w.T + group_bias
        g_idx = jnp.argmax(g_logits, axis=-1)
        e_logits = (flat @ expert_gate_w.T).reshape(S, G, EG)
        e_sel = jnp.take_along_axis(e_logits, g_idx[:, None, None], axis=1)[:, 0, :]
        e_sel = e_sel + expert_bias.reshape(G, EG)[g_idx]
        e_probs = jax.nn.softmax(e_sel, axis=-1)
        topv, topi = jax.lax.top_k(e_probs, K)
        topv = topv / (topv.sum(-1, keepdims=True) + 1e-08)
        disp = g_idx[:, None] * EG + topi
        h_expert = _swiglu(flat @ expert_in_w.T)
        rows = jnp.arange(S)[:, None]
        comb = jnp.zeros((S, E), flat.dtype).at[rows, disp].add(topv)
        cnt = jnp.zeros((S, E), flat.dtype).at[rows, disp].add(1.0)
        routed = cnt @ expert_out_bias
        for e in range(E):
            routed = routed + comb[:, e:e + 1] * (h_expert @ expert_out_weight[e].T)
        return (out_shared + routed).reshape(Bx, Tx, Cx)
    h = _L0_tok_ref(x, L0_tok_W)
    h = h + _L0_attn_ref(_layernorm(h, axis=-1), L0_attn_Wq, L0_attn_bq, L0_attn_Wk, L0_attn_bk, L0_attn_Wv, L0_attn_bv, L0_attn_Wo, L0_attn_bo)
    h = h + _L0_ffn_ref(_layernorm(h, axis=-1), L0_ffn_ln_scale, L0_ffn_ln_bias, L0_ffn_shared_in_w, L0_ffn_shared_out_w, L0_ffn_shared_out_b, L0_ffn_expert_in_w, L0_ffn_expert_out_weight, L0_ffn_expert_out_bias, L0_ffn_group_gate_w, L0_ffn_expert_gate_w, L0_ffn_group_bias, L0_ffn_expert_bias)
    return h

_drawn_inputs = setup_inputs


def setup_inputs(seed=0):
    import zlib

    import numpy as np

    out = dict(_drawn_inputs(seed))
    spreads = {'L0_ffn_ln_scale': (1.0, 0.2),
     'L0_ffn_ln_bias': (0.0, 0.1),
     'L0_ffn_shared_out_b': (0.0, 0.283),
     'L0_ffn_expert_out_bias': (0.0, 0.1),
     'L0_ffn_group_bias': (0.0, 0.1),
     'L0_ffn_expert_bias': (0.0, 0.1)}
    factors = {'L0_attn_bq': 7.963,
     'L0_attn_bk': 64.0,
     'L0_ffn_shared_in_w': 5.006,
     'L0_ffn_shared_out_w': 4.85,
     'L0_ffn_expert_in_w': 7.006,
     'L0_ffn_expert_out_weight': 7.197}
    for name, (base, spread) in spreads.items():
        noise = np.random.default_rng([zlib.crc32(name.encode()), seed]).standard_normal(out[name].shape)
        drawn = base * np.exp(spread * noise) if base else spread * noise
        out[name] = jnp.asarray(drawn.astype(out[name].dtype))
    for name, factor in factors.items():
        out[name] = (out[name] * factor).astype(out[name].dtype)
    return out
```

```python
from contextlib import ExitStack

import numpy as np
import concourse.bass as bass
from concourse import mybir

F32 = mybir.dt.float32
F32R = mybir.dt.float32r
ALU = mybir.AluOpType
ACT = mybir.ActivationFunctionType
AX = mybir.AxisListType

P = 128
B, S, F = 8, 1024, 29
TILES = S // P
HALF = 512
HT = HALF // P
HEADS, DH = 8, 16
G4 = 4
HID = 256
EXPERTS, GROUPS, EG = 8, 2, 4
NGATE = GROUPS + EXPERTS
ODD = 64
STACK = ODD + 3 * DH
SHIFT = P - 2
EPS = 1e-5
MASK = -100000.0
VW = 32

UNITS = [(0, 0), (0, 1), (1, 1), (1, 0)]
SCORE_STEPS = [(u, HT * half + t, j) for u, (g, half) in enumerate(UNITS) for t in range(HT) for j in range(G4)]
PROB_STEPS = [(u, kt) for u, (g, half) in enumerate(UNITS) for kt in range(HT * (half + 1))]
NS, NP_, NU = len(SCORE_STEPS), len(PROB_STEPS), len(UNITS)
UNIT_S = NS // NU
DIAG = [k for k, (u, kt) in enumerate(PROB_STEPS) if kt >= HT * UNITS[u][1]]
LAST_OF_UNIT = {max(k for k, (u, _) in enumerate(PROB_STEPS) if u == v): v for v in range(NU)}
MAX_LAG = 3
PROB_LAG = 7
PT_SLOTS = 2


def prob_columns(k):
    u, kt = PROB_STEPS[k]
    q0 = max(0, kt * P - UNITS[u][1] * HALF)
    return q0, min(q0, HALF - 256)


def later(i):
    return not (isinstance(i, int) and i == 0)


def attention_order():
    order, s, k, turned = [], 0, 0, 0
    vector_t = scalar_t = 0.0
    while s < NS or k < NP_:
        if turned < NU and (s >= min(NS, UNIT_S * (turned + 1) + MAX_LAG)):
            order.append(("turn", turned))
            turned += 1
            continue
        ready = k < NP_ and s >= min(NS, UNIT_S * (PROB_STEPS[k][0] + 1) + PROB_LAG)
        if ready and (scalar_t <= vector_t or s == NS):
            order.append(("prob", k))
            scalar_t += 4 * ((HALF - prob_columns(k)[0]) / 1.2 + 51)
            k += 1
        else:
            if not ready:
                scalar_t = max(scalar_t, vector_t)
            order.append(("score", s))
            vector_t += (SCORE_STEPS[s][1] + 1) * P * 1.05 + 77
            s += 1
    return order


ATTENTION = attention_order()
FRONT = [("emb",), ("turn1", 0), ("turn1", 1), ("qk", 0), ("qk", 1), ("v",)]
TAIL = [("in", 0), ("route",), ("in", 1), ("in", 2), ("in", 3), ("in", 4), ("counts", 0), ("in", 5), ("counts", 1),
        ("in", 6), ("in", 7), ("shared", 0), ("expert", 0), ("expert", 1), ("expert", 2), ("expert", 3),
        ("shared", 1), ("expert", 4), ("expert", 5), ("expert", 6), ("expert", 7)]
WOVEN = {("in", 3): [("emb",)], ("expert", 0): [("turn1", 0), ("turn1", 1)], ("expert", 1): [("qk", 0)],
         ("expert", 2): [("qk", 1)], ("expert", 3): [("v",)]}
IN_STEPS = [(kind, c, half) for half in range(2) for kind in (1, 0) for c in range(HID // P)]


def woven_tail(with_front):
    out = []
    for st in TAIL:
        out.append((st, 0))
        if with_front:
            out += [(f, 1) for f in WOVEN.get(st, [])]
    return out


def build(nc, x_t, tok_w, pos, wq, wk, wv, wo, bq, bk, bv, bo, ln_s, ln_b, w_in, w_shared, w_expert, w_bias,
          w_gate, b_gate, out):
    with ExitStack() as ctx:
        def sb(name, shape, dt=F32):
            return ctx.enter_context(nc.sbuf_tensor(name, shape, dt))

        def sem(name):
            return ctx.enter_context(nc.semaphore(name))

        bank = [ctx.enter_context(nc.psum_tensor(f"bank{n}", [P, HALF], F32)) for n in (4, 5, 6, 7)]
        pair = [ctx.enter_context(nc.psum_tensor(f"pair{n}", [P, 2 * HALF], F32)) for n in range(2)]
        b4, b5, b6, b7 = bank

        ident = sb("ident", [P, P])
        causal = sb("causal", [P, S])
        tri = sb("tri", [P, EG * EG])
        half_pow = sb("half_pow", [P, TILES])
        minus1 = sb("minus1", [2, S], F32R)
        pos_sb = sb("pos_sb", [P, TILES, P])
        tokw_sb = sb("tokw_sb", [F, P])
        wq_sb, wk_sb, wv_sb, wo_sb = (sb(n, [P, P]) for n in ("wq_sb", "wk_sb", "wv_sb", "wo_sb"))
        wqk_h = sb("wqk_h", [P, 2, P], F32R)
        wqk_l = sb("wqk_l", [P, 2, P], F32R)
        bq_sb, bk_sb, lns_sb, lnb_sb = (sb(n, [P, 1]) for n in ("bq_sb", "bk_sb", "lns_sb", "lnb_sb"))
        bv_sb, bo_sb = sb("bv_sb", [P, P]), sb("bo_sb", [P, P])
        bgate_sb = sb("bgate_sb", [P, NGATE])
        wgate_sb = sb("wgate_sb", [P, NGATE])
        wbias_sb = sb("wbias_sb", [EXPERTS + 1, P])
        wshared_sb = sb("wshared_sb", [P, HID // P, P])
        win_h, win_l = sb("win_h", [P, 4 * HID], F32R), sb("win_l", [P, 4 * HID], F32R)
        wex_h = sb("wex_h", [P, HID // P, EXPERTS * P], F32R)
        wex_l = sb("wex_l", [P, HID // P, EXPERTS * P], F32R)

        x_sb = sb("x_sb", [F, S])
        h = sb("h", [P, TILES, P])
        hb = sb("hb", [P, TILES, P])
        stats = sb("stats", [P, TILES, 6])
        mv = sb("mv", [P, TILES, 2])
        var1 = sb("var1", [P, TILES])
        rs1 = sb("rs1", [P, TILES])
        z = sb("z", [P, TILES, P])
        zt = sb("zt", [P, S])
        zt_h, zt_l = sb("zt_h", [P, S], F32R), sb("zt_l", [P, S], F32R)
        qk_h, qk_l = sb("qk_h", [P, 2, S], F32R), sb("qk_l", [P, 2, S], F32R)
        v = sb("v", [P, TILES, HEADS, VW])
        q_stack = sb("q_stack", [P, HEADS, S], F32R)
        k_stack = sb("k_stack", [P, HEADS // 2, S], F32R)
        mx = sb("mx", [P, NS])
        mrow_h, mrow_l = sb("mrow_h", [UNIT_S, NU, P], F32R), sb("mrow_l", [UNIT_S, NU, P], F32R)
        pt = sb("pt", [P, PT_SLOTS, G4, HALF])
        wex_sb = pt[:, 0, :, :].rearrange("p (c x) q -> p c (x q)", c=HID // P)
        win_sb = pt[:, 1, 0:2, :].rearrange("p x q -> p (x q)")
        ot = sb("ot", [P, 2, S])
        qk = ot
        rec = sb("rec", [P, TILES, HEADS])
        an, ant = z, zt
        h2 = sb("h2", [P, TILES, P])
        stats2 = sb("stats2", [P, TILES, 6])
        mv2 = sb("mv2", [P, TILES, 2])
        t1, t2, t3, t4, t5, t6 = (sb(f"ln_{n}", [P, TILES]) for n in range(6))
        t4e = sb("ln_4e", [P, TILES])
        z2, z2t, z2t_h, z2t_l = z, zt, zt_h, zt_l
        gl = sb("gl", [P, TILES, NGATE])
        gm = sb("gm", [P, TILES, GROUPS])
        both = sb("both", [P, TILES, GROUPS, EG])
        esel = sb("esel", [P, TILES, EG])
        emax = sb("emax", [P, TILES])
        esub = sb("esub", [P, TILES, EG])
        eprob = sb("eprob", [P, TILES, EG])
        esum, erec = sb("esum", [P, TILES]), sb("erec", [P, TILES])
        pn = sb("pn", [P, TILES, EG])
        cmp_gt, cmp_eq = sb("cmp_gt", [P, TILES, EG * EG]), sb("cmp_eq", [P, TILES, EG * EG])
        cmp_tie, cmp_all = sb("cmp_tie", [P, TILES, EG * EG]), sb("cmp_all", [P, TILES, EG * EG])
        rank = sb("rank", [P, TILES * EG])
        top = sb("top", [P, TILES, EG])
        topp = sb("topp", [P, TILES, EG])
        tsum, tden, trec = sb("tsum", [P, TILES]), sb("tden", [P, TILES]), sb("trec", [P, TILES])
        wsel = sb("wsel", [P, TILES, EG])
        comb = sb("comb", [P, TILES, GROUPS, EG])
        cnt = sb("cnt", [P, TILES, EXPERTS + 1])
        cnt_t = sb("cnt_t", [EXPERTS + 1, S])
        th = sb("th", [P, 2, HALF])
        gate = sb("gate", [P, HALF])
        hid = pt[:].rearrange("p s j q -> p (s j q)").rearrange("p (k c n) -> p k c n", k=2, c=HID // P)
        hid_h = sb("hid_h", [P, HID // P, S], F32R)
        hid_l = sb("hid_l", [P, HID // P, S], F32R)
        acc = h2

        w_in1 = sem("w_front_loaded")
        w_in2 = sem("w_rest_loaded")
        const_made = sem("const_made")
        ones_in = sem("minus_ones_in_stack")
        wsplit_qk = sem("wsplit_qk")
        wsplit_h = sem("wsplit_h")
        wsplit_l = sem("wsplit_l")
        x_in = sem("x_in")
        front_mm = sem("front_mm")
        h_made = sem("h_made")
        hb_made = sem("hb_made")
        stat1 = sem("stat1")
        mv_made = sem("mv_made")
        var_made = sem("var_made")
        rs_made = sem("rs_made")
        z_made = sem("z_made")
        front_act = sem("front_act")
        zth_made, ztl_made = sem("zth_made"), sem("ztl_made")
        qkh_made, qkl_made = sem("qkh_made"), sem("qkl_made")
        v_made = sem("v_made")
        stack_in = [sem("stack_in_g0"), sem("stack_in_g1")]
        s_ready, s_taken = sem("scores_ready"), sem("scores_taken")
        m_turned, mh_made, ml_made, m_in = sem("max_turned"), sem("mh_made"), sem("ml_made"), sem("max_in_stack")
        st_ready, exp_done, mask_done = sem("st_ready"), sem("exp_done"), sem("mask_done")
        pv_done, pv_taken = sem("pv_done"), sem("pv_taken")
        to_ready, rec_made, an_made = sem("to_ready"), sem("rec_made"), sem("an_made")
        ant_ready, ant_made = sem("ant_ready"), sem("ant_made")
        o_ready, h2_made = sem("o_ready"), sem("h2_made")
        stat2, mv2_made, ln2_step, z2_made = sem("stat2"), sem("mv2_made"), sem("ln2_step"), sem("z2_made")
        z2t_ready, z2t_made = sem("z2t_ready"), sem("z2t_made")
        z2h_made, z2l_made = sem("z2h_made"), sem("z2l_made")
        gl_ready, route_step, eexp_done = sem("gl_ready"), sem("route_step"), sem("eexp_done")
        in_ready, tanh_done, gate_made, hid_made = sem("in_ready"), sem("tanh_done"), sem("gate_made"), sem("hid_made")
        hidh_made, hidl_made = sem("hidh_made"), sem("hidl_made")
        cnt_ready, cnt_taken = sem("cnt_ready"), sem("cnt_taken")
        shared_ready, base_made = sem("shared_ready"), sem("base_made")
        ex_ready, ex_step = sem("ex_ready"), sem("ex_step")
        out_done = sem("out_done")
        wsel_made = sem("wsel_made")
        ln2_mid = sem("ln2_mid")
        sem_zero = sem("sem_zero")
        went_on = sem("went_on")

        out_v = out.rearrange("b (t p) c -> b p t c", p=P)
        CONSTS = 7
        ROUTE = 20

        def halfs(half):
            return slice(half * HALF, (half + 1) * HALF)

        def tiles(half):
            return slice(half * HT, (half + 1) * HT)

        def words(ap):
            return ap.bitcast(F32)

        def alone(eng, semaphore, value):
            eng.wait_ge(semaphore, value)
            eng.sem_inc(went_on, 1)

        block = ctx.enter_context(nc.Block())

        @block.sync
        def _(sp):
            def load_x(i):
                sp.dma_start(x_sb[:], x_t[:, bass.ds(i * S, S)]).then_inc(x_in, 16)

            load_x(0)
            for dst, src in ((tokw_sb, tok_w), (pos_sb, pos), (wq_sb, wq), (wk_sb, wk), (bq_sb, bq), (bk_sb, bk),
                             (wv_sb, wv), (bv_sb, bv), (bo_sb, bo)):
                sp.dma_start(dst[:], src).then_inc(w_in1, 16)
            for dst, src in ((wo_sb, wo), (lns_sb, ln_s), (lnb_sb, ln_b), (win_sb, w_in), (wshared_sb, w_shared),
                             (wex_sb, w_expert), (wbias_sb, w_bias), (wgate_sb, w_gate), (bgate_sb, b_gate)):
                sp.dma_start(dst if dst is win_sb or dst is wex_sb else dst[:], src).then_inc(w_in2, 16)
            sp.wait_ge(const_made, CONSTS)
            for n in range(HEADS // 2):
                sp.dma_start(words(k_stack[SHIFT:P, n, :]), words(minus1[:])).then_inc(ones_in, 16)

            def stacks(i, more):
                sp.wait_ge(qkh_made, i * 4 + 4)
                sp.wait_ge(qkl_made, i * 4 + 4)
                if more:
                    load_x(i + 1)
                for hd in range(HEADS):
                    rows = slice(hd * DH, (hd + 1) * DH)
                    for n, (qp, kp) in enumerate(((qk_h, qk_h), (qk_h, qk_l), (qk_l, qk_h))):
                        to = slice(hd % 2 * ODD + n * DH, hd % 2 * ODD + (n + 1) * DH)
                        sp.dma_start(words(q_stack[to, hd, :]), words(qp[rows, 0, :])).then_inc(stack_in[hd // G4], 16)
                        sp.dma_start(words(k_stack[to, hd // 2, :]), words(kp[rows, 1, :])).then_inc(stack_in[hd // G4], 16)

            def maxima(i):
                for u, (g, half) in enumerate(UNITS):
                    sp.wait_ge(ml_made, i * NU + u + 1)
                    for row, part in ((SHIFT, mrow_h), (SHIFT + 1, mrow_l)):
                        for j in range(G4):
                            dst = q_stack[row:row + 1, g * G4 + j, halfs(half)].rearrange("a (t q) -> a t q", q=P)
                            sp.dma_start(words(dst), words(part[j * HT:(j + 1) * HT, u, :])).then_inc(m_in, 16)

            def stores(i):
                for half in range(2):
                    sp.wait_ge(ex_step, i * TILES * EXPERTS + (half + 1) * HT * EXPERTS)
                    sp.dma_start(out_v[i, :, tiles(half), :], acc[:, tiles(half), :]).then_inc(out_done, 16)

            stacks(0, True)
            maxima(0)
            stacks(1, True)
            stores(0)
            with sp.Fori(1, B - 2) as i:
                maxima(i)
                stacks(i + 1, True)
                stores(i)
            maxima(B - 2)
            stacks(B - 1, False)
            stores(B - 2)
            maxima(B - 1)
            stores(B - 1)
            sp.wait_ge(out_done, B * 2 * 16)

        @block.tensor
        def _(pe):
            def split_mm(dst, wh, wl, xh, xl, first=True, last=True):
                nc.tensor.matmul(dst, wh, xh, start=first, stop=False)
                nc.tensor.matmul(dst, wl, xh, start=False, stop=False)
                return nc.tensor.matmul(dst, wh, xl, start=False, stop=last)

            def front(i, st):
                kind = st[0]
                if kind == "emb":
                    pe.wait_ge(x_in, (i + 1) * 16)
                    for half, dst in ((0, b6), (1, b7)):
                        for t in range(HT):
                            mm = nc.tensor.matmul(dst[:, t * P:(t + 1) * P],
                                                  x_sb[:, (half * HT + t) * P:(half * HT + t + 1) * P],
                                                  tokw_sb[:], start=True, stop=True)
                        mm.then_inc(front_mm, 1)
                if kind == "turn1":
                    half = st[1]
                    pe.wait_ge(z_made, i * TILES + (half + 1) * HT)
                    for t in range(HT):
                        mm = nc.tensor.transpose((b6, b7)[half][:, t * P:(t + 1) * P], z[:, half * HT + t, :], ident[:])
                    mm.then_inc(front_mm, 1)
                if kind == "qk":
                    half = st[1]
                    pe.wait_ge(zth_made, i * 2 + half + 1)
                    pe.wait_ge(ztl_made, i * 2 + half + 1)
                    for w, dst in ((0, b6), (1, b7)):
                        pe.wait_ge(front_act, i * 6 + 2 * half + w + 1)
                        split_mm(dst[:], wqk_h[:, w, :], wqk_l[:, w, :], zt_h[:, halfs(half)],
                                 zt_l[:, halfs(half)]).then_inc(front_mm, 1)
                if kind == "v":
                    for half, dst in ((0, b6), (1, b7)):
                        pe.wait_ge(front_act, i * 6 + 5 + half)
                        for t in range(HT):
                            mm = nc.tensor.matmul(dst[:, t * P:(t + 1) * P],
                                                  zt[:, (half * HT + t) * P:(half * HT + t + 1) * P],
                                                  wv_sb[:], start=True, stop=True)
                        mm.then_inc(front_mm, 1)

            def score(i, s):
                u, t, j = SCORE_STEPS[s]
                hd = UNITS[u][0] * G4 + j
                if s == 0:
                    pe.wait_ge(stack_in[0], (i + 1) * 384)
                    if later(i):
                        pe.wait_ge(ex_step, i * TILES * EXPERTS)
                if s == 2 * UNIT_S:
                    pe.wait_ge(stack_in[1], (i + 1) * 384)
                if s >= 2:
                    pe.wait_ge(s_taken, i * NS + s - 1)
                n = max(256, (t + 1) * P)
                cuts = [0, n] if n <= HALF else [0, HALF if n >= HALF + 256 else HALF - P, n]
                for a, b in zip(cuts, cuts[1:]):
                    for c, d in ([(a, b)] if a >= HALF or b <= HALF else [(a, HALF), (HALF, b)]):
                        mm = nc.tensor.matmul(pair[s % 2][:, c:d], q_stack[0:STACK, hd, t * P:(t + 1) * P],
                                              k_stack[0:STACK, hd // 2, c:d], start=True, stop=True)
                mm.then_inc(s_ready, 1)

            def turn(i, u):
                if u == 0:
                    pe.wait_ge(v_made, i * 2 + 2)
                else:
                    pe.wait_ge(ml_made, i * NU + u)
                pe.wait_ge(s_taken, i * NS + (u + 1) * UNIT_S)
                nc.tensor.transpose(b7[0:UNIT_S, 0:P], mx[:, u * UNIT_S:(u + 1) * UNIT_S], ident[:]).then_inc(m_turned, 1)

            def prob(i, k):
                u, kt = PROB_STEPS[k]
                g, half = UNITS[u]
                q0, c0 = prob_columns(k)
                if kt == 0:
                    pe.wait_ge(m_in, i * NU * 128 + (u + 1) * 128)
                if k == 0:
                    if later(i):
                        pe.wait_ge(base_made, i * 2)
                for j in range(G4):
                    p = k * G4 + j
                    if p >= 2:
                        pe.wait_ge(exp_done, i * NP_ * G4 + p - 1)
                    hd = g * G4 + j
                    nc.tensor.matmul((b4, b5)[p % 2][:, c0:HALF], k_stack[:, hd // 2, kt * P:(kt + 1) * P],
                                     q_stack[:, hd, half * HALF + c0:(half + 1) * HALF],
                                     start=True, stop=True).then_inc(st_ready, 1)

            def weigh(i, k):
                u, kt = PROB_STEPS[k]
                g, half = UNITS[u]
                q0, _ = prob_columns(k)
                pe.wait_ge(exp_done, i * NP_ * G4 + (k + 1) * G4)
                if k in DIAG:
                    pe.wait_ge(mask_done, i * len(DIAG) + DIAG.index(k) + 1)
                if kt == 0 and u == 0:
                    pe.wait_ge(v_made, i * 2 + 2)
                if kt == 0 and u > 0:
                    pe.wait_ge(pv_taken, i * NU + u)
                for j in range(G4):
                    mm = nc.tensor.matmul(b6[32 * j:32 * j + VW, q0:HALF], v[:, kt, g * G4 + j, :],
                                          pt[:, k % PT_SLOTS, j, q0:HALF], start=(kt == 0),
                                          stop=(kt == HT * (half + 1) - 1), tile_position=(0, 32 * j))
                mm.then_inc(pv_done, 1)

            def attention(i):
                weighed = 0
                for what, n in ATTENTION:
                    if what == "score":
                        score(i, n)
                    elif what == "turn":
                        turn(i, n)
                    else:
                        prob(i, n)
                        if n >= 1:
                            weigh(i, n - 1)
                weigh(i, NP_ - 1)

            def post(i):
                pe.wait_ge(s_taken, (i + 1) * NS)
                for n in range(HT):
                    if n == 0:
                        pe.wait_ge(pv_taken, (i + 1) * NU)
                    for t in (2 * n, 2 * n + 1):
                        for g in range(2):
                            to = (n % 2) * HALF + (t % 2) * 256 + g * P
                            mm = nc.tensor.transpose(pair[n // 2][:, to:to + P], ot[:, g, t * P:(t + 1) * P], ident[:])
                    mm.then_inc(to_ready, 1)
                pe.wait_ge(exp_done, (i + 1) * NP_ * G4)
                for half, dst in ((0, b4), (1, b5)):
                    pe.wait_ge(an_made, i * HT + 2 * half + 2)
                    for t in range(HT):
                        mm = nc.tensor.transpose(dst[:, t * P:(t + 1) * P], an[:, half * HT + t, :], ident[:])
                    mm.then_inc(ant_ready, 1)
                pe.wait_ge(ml_made, (i + 1) * NU)
                for half, dst in ((0, b6), (1, b7)):
                    pe.wait_ge(ant_made, i * 2 + half + 1)
                    for t in range(HT):
                        tt = half * HT + t
                        mm = nc.tensor.matmul(dst[:, t * P:(t + 1) * P], ant[:, tt * P:(tt + 1) * P], wo_sb[:],
                                              start=True, stop=True)
                    mm.then_inc(o_ready, 1)
                for half, dst in ((0, b4), (1, b5)):
                    pe.wait_ge(z2_made, i * TILES + (half + 1) * HT)
                    for t in range(HT):
                        mm = nc.tensor.transpose(dst[:, t * P:(t + 1) * P], z2[:, half * HT + t, :], ident[:])
                    mm.then_inc(z2t_ready, 1)
                pe.wait_ge(h2_made, i * 2 + 2)
                pe.wait_ge(z2t_made, i * 2 + 2)
                for t in range(TILES):
                    mm = nc.tensor.matmul(b6[:, t * NGATE:(t + 1) * NGATE], z2t[:, t * P:(t + 1) * P], wgate_sb[:],
                                          start=True, stop=True)
                mm.then_inc(gl_ready, 1)

            def tail(i, st):
                kind = st[0]
                if kind == "in":
                    q = st[1]
                    ex, c, half = IN_STEPS[q]
                    if q % 4 == 0:
                        pe.wait_ge(z2h_made, i * 2 + half + 1)
                        pe.wait_ge(z2l_made, i * 2 + half + 1)
                    if q == 0:
                        pe.wait_ge(an_made, (i + 1) * HT)
                    if q >= 2:
                        pe.wait_ge(hid_made, i * 8 + q - 1)
                    for ab in range(2):
                        w0 = ex * 2 * HID + ab * HID + c * P
                        mm = split_mm(pair[q % 2][:, ab * HALF:(ab + 1) * HALF], win_h[:, w0:w0 + P],
                                      win_l[:, w0:w0 + P], z2t_h[:, halfs(half)], z2t_l[:, halfs(half)])
                    mm.then_inc(in_ready, 1)
                if kind == "counts":
                    half = st[1]
                    if half == 0:
                        pe.wait_ge(route_step, (i + 1) * ROUTE)
                    else:
                        pe.wait_ge(cnt_taken, i * 2 + 1)
                    for t in range(HT):
                        mm = nc.tensor.transpose(b5[0:EXPERTS + 1, t * P:(t + 1) * P], cnt[:, half * HT + t, :], ident[:])
                    mm.then_inc(cnt_ready, 1)
                if kind == "shared":
                    half = st[1]
                    pe.wait_ge(hid_made, i * 8 + 8)
                    pe.wait_ge(cnt_taken, i * 2 + 2)
                    for t in range(HT):
                        tt = half * HT + t
                        dst = (b4, b5)[half][:, t * P:(t + 1) * P]
                        for c in range(HID // P):
                            nc.tensor.matmul(dst, hid[:, 0, c, tt * P:(tt + 1) * P], wshared_sb[:, c, :],
                                             start=(c == 0), stop=False)
                        mm = nc.tensor.matmul(dst, cnt_t[:, tt * P:(tt + 1) * P], wbias_sb[:], start=False, stop=True)
                    mm.then_inc(shared_ready, 1)
                if kind == "expert":
                    t = st[1]
                    if t == 0:
                        pe.wait_ge(hidl_made, i * 4 + 4)
                        pe.wait_ge(hidh_made, i * 4 + 4)
                    if t >= 2:
                        pe.wait_ge(ex_step, (i * TILES + t - 1) * EXPERTS)
                    tok = slice(t * P, (t + 1) * P)
                    for g in range(GROUPS):
                        dst = pair[t % 2][:, g * HALF:(g + 1) * HALF]
                        w = slice(g * HALF, (g + 1) * HALF)
                        for c in range(HID // P):
                            nc.tensor.matmul(dst, hid_h[:, c, tok], wex_h[:, c, w], start=(c == 0), stop=False)
                            nc.tensor.matmul(dst, hid_h[:, c, tok], wex_l[:, c, w], start=False, stop=False)
                            mm = nc.tensor.matmul(dst, hid_l[:, c, tok], wex_h[:, c, w], start=False,
                                                  stop=(c == HID // P - 1))
                    mm.then_inc(ex_ready, 1)

            def image(i, another=True):
                attention(i)
                post(i)
                for st, nxt in woven_tail(another):
                    front(i + 1, st) if nxt else tail(i, st)

            pe.wait_ge(w_in1, 9 * 16)
            pe.wait_ge(const_made, CONSTS)
            front(0, FRONT[0])
            pe.wait_ge(wsplit_qk, 4)
            for st in FRONT[1:]:
                front(0, st)
            pe.wait_ge(ones_in, HEADS // 2 * 16)
            pe.wait_ge(w_in2, 9 * 16)
            pe.wait_ge(wsplit_h, 2)
            pe.wait_ge(wsplit_l, 2)
            image(0)
            with pe.Fori(1, B - 1) as i:
                image(i)
            image(B - 1, False)

        @block.vector
        def _(dve):
            dve.wait_ge(w_in1, 9 * 16)
            for n, w in enumerate((wq_sb, wk_sb)):
                nc.vector.tensor_copy(wqk_h[:, n, :], w[:]).then_inc(wsplit_qk, 1)
            dve.wait_ge(wsplit_qk, 2)
            for n, w in enumerate((wq_sb, wk_sb)):
                nc.vector.tensor_tensor(wqk_l[:, n, :], w[:], wqk_h[:, n, :].bitcast(F32),
                                        ALU.subtract).then_inc(wsplit_qk, 1)

            def front(i, st):
                kind = st[0]
                if kind == "emb":
                    for half, src in ((0, b6), (1, b7)):
                        dve.wait_ge(front_mm, i * 10 + half + 1)
                        nc.vector.tensor_tensor(h[:, tiles(half), :], src[:].rearrange("p (t c) -> p t c", c=P),
                                                pos_sb[:, tiles(half), :], ALU.add).then_inc(h_made, 1)
                    for half in range(2):
                        dve.wait_ge(h_made, i * 2 + half + 1)
                        for t in range(half * HT, (half + 1) * HT):
                            nc.vector.bn_stats(stats[:, t, :], h[:, t, :]).then_inc(stat1, 1)
                    alone(dve, stat1, (i + 1) * TILES)
                    for t in range(TILES):
                        nc.vector.bn_aggr(mv[:, t, :], stats[:, t, :]).then_inc(mv_made, 1)
                if kind == "turn1":
                    half = st[1]
                    if half == 0:
                        dve.wait_ge(rs_made, i + 1)
                        for t in range(TILES):
                            nc.vector.tensor_scalar(z[:, t, :], h[:, t, :], mv[:, t, 0:1], rs1[:, t:t + 1],
                                                    ALU.subtract, ALU.mult).then_inc(z_made, 1)
                if kind == "qk":
                    half = st[1]
                    for w in range(2):
                        dve.wait_ge(front_act, i * 6 + 3 + 2 * half + w)
                        nc.vector.tensor_copy(qk_h[:, w, halfs(half)], qk[:, w, halfs(half)]).then_inc(qkh_made, 1)
                if kind == "v":
                    for half, src in ((0, b6), (1, b7)):
                        dve.wait_ge(front_mm, i * 10 + 9 + half)
                        for t in range(HT):
                            dst = v[:, half * HT + t, :, 0:DH]
                            ins = nc.vector.tensor_tensor(
                                dst, src[:, t * P:(t + 1) * P].rearrange("p (h d) -> p h d", d=DH),
                                bv_sb[:].rearrange("p (h d) -> p h d", d=DH), ALU.add)
                        ins.then_inc(v_made, 1)
                if kind == "turn1":
                    half = st[1]
                    dve.wait_ge(front_act, i * 6 + half + 1)
                    nc.vector.tensor_copy(zt_h[:, halfs(half)], zt[:, halfs(half)]).then_inc(zth_made, 1)

            def maxima_split(i, u):
                dve.wait_ge(m_turned, i * NU + u + 1)
                nc.vector.tensor_copy(mrow_h[:, u, :], b7[0:UNIT_S, 0:P]).then_inc(mh_made, 1)
                dve.wait_ge(mh_made, i * NU + u + 1)
                nc.vector.tensor_tensor(mrow_l[:, u, :], b7[0:UNIT_S, 0:P], mrow_h[:, u, :].bitcast(F32),
                                        ALU.subtract).then_inc(ml_made, 1)

            def attention(i):
                split = 0
                for s in range(NS + 1):
                    if split < NU and s >= min(NS, UNIT_S * (split + 1) + MAX_LAG):
                        maxima_split(i, split)
                        split += 1
                    if s == NS:
                        break
                    u, t, j = SCORE_STEPS[s]
                    n = (t + 1) * P
                    col = u * UNIT_S + j * HT + t % HT
                    alone(dve, s_ready, i * NS + s + 1)
                    src = pair[s % 2][:, 0:n]
                    nc.vector.tensor_tensor_reduce(src, src, causal[:, S - n:S], 1.0, -3.0e38, ALU.add, ALU.max,
                                                   mx[:, col:col + 1]).then_inc(s_taken, 1)

            def post(i):
                for n in range(HT):
                    dve.wait_ge(to_ready, i * HT + n + 1)
                    src = pair[n // 2][:, (n % 2) * HALF:(n % 2 + 1) * HALF].rearrange("p (k w) -> p k w", w=VW)
                    rc = rec[:, 2 * n:2 * n + 2, :].rearrange("p t h -> p (t h)")
                    nc.vector.reciprocal(rc, src[:, :, DH]).then_inc(rec_made, 1)
                    dve.wait_ge(rec_made, i * HT + n + 1)
                    nc.vector.tensor_tensor(an[:, 2 * n:2 * n + 2, :].rearrange("p t (h d) -> p (t h) d", d=DH),
                                            src[:, :, 0:DH], rc.unsqueeze(2).to_broadcast([P, 2 * HEADS, DH]),
                                            ALU.mult).then_inc(an_made, 1)
                dve.wait_ge(hb_made, i + 1)
                if later(i):
                    dve.wait_ge(out_done, i * 32)
                for half, src in ((0, b6), (1, b7)):
                    dve.wait_ge(o_ready, i * 2 + half + 1)
                    nc.vector.tensor_tensor(h2[:, tiles(half), :], src[:].rearrange("p (t c) -> p t c", c=P),
                                            hb[:, tiles(half), :], ALU.add).then_inc(h2_made, 1)
                for half in range(2):
                    dve.wait_ge(h2_made, i * 2 + half + 1)
                    for t in range(half * HT, (half + 1) * HT):
                        nc.vector.bn_stats(stats2[:, t, :], h2[:, t, :]).then_inc(stat2, 1)
                alone(dve, stat2, (i + 1) * TILES)
                for t in range(TILES):
                    nc.vector.bn_aggr(mv2[:, t, :], stats2[:, t, :]).then_inc(mv2_made, 1)
                dve.wait_ge(ln2_step, (i + 1) * 6)
                for t in range(TILES):
                    nc.vector.tensor_scalar(z2[:, t, :], h2[:, t, :], mv2[:, t, 0:1], t6[:, t:t + 1],
                                            ALU.subtract, ALU.mult).then_inc(z2_made, 1)
                for half in range(2):
                    dve.wait_ge(z2t_made, i * 2 + half + 1)
                    nc.vector.tensor_copy(z2t_h[:, halfs(half)], z2t[:, halfs(half)]).then_inc(z2h_made, 1)

            def route(i):
                step = [0]

                def then(ins):
                    ins.then_inc(route_step, 1)
                    step[0] += 1
                    dve.wait_ge(route_step, i * ROUTE + step[0])

                def outer(ap, by):
                    a = ap.unsqueeze(3 if by == "i" else 2)
                    return a.to_broadcast([P, TILES, EG, EG])

                def sq(ap):
                    return ap.rearrange("p t (i j) -> p t i j", j=EG)

                dve.wait_ge(gl_ready, i + 1)
                then(nc.vector.tensor_tensor(gl[:], b6[:, 0:TILES * NGATE].rearrange("p (t n) -> p t n", n=NGATE),
                                             bgate_sb[:].unsqueeze(1).to_broadcast([P, TILES, NGATE]), ALU.add))
                then(nc.vector.tensor_tensor(gm[:, :, 0:1], gl[:, :, 1:2], gl[:, :, 0:1], ALU.is_le))
                then(nc.vector.tensor_tensor(gm[:, :, 1:2], gl[:, :, 1:2], gl[:, :, 0:1], ALU.is_gt))
                gmb = gm[:].unsqueeze(3).to_broadcast([P, TILES, GROUPS, EG])
                then(nc.vector.tensor_tensor(both[:], gl[:, :, GROUPS:].rearrange("p t (g e) -> p t g e", e=EG),
                                             gmb, ALU.mult))
                then(nc.vector.tensor_tensor(esel[:], both[:, :, 0, :], both[:, :, 1, :], ALU.add))
                then(nc.vector.tensor_reduce(emax[:], esel[:], AX.X, ALU.max))
                then(nc.vector.tensor_tensor(esub[:], esel[:], emax[:].unsqueeze(2).to_broadcast([P, TILES, EG]),
                                             ALU.subtract))
                then(nc.vector.tensor_tensor(sq(cmp_gt[:]), outer(esel[:], "j"), outer(esel[:], "i"), ALU.is_gt))
                then(nc.vector.tensor_tensor(sq(cmp_eq[:]), outer(esel[:], "j"), outer(esel[:], "i"), ALU.is_equal))
                then(nc.vector.tensor_tensor(cmp_tie[:], cmp_eq[:], tri[:].unsqueeze(1).to_broadcast(
                    [P, TILES, EG * EG]), ALU.mult))
                then(nc.vector.tensor_tensor(cmp_all[:], cmp_gt[:], cmp_tie[:], ALU.add))
                then(nc.vector.tensor_reduce(rank[:], cmp_all[:].rearrange("p t (i j) -> p (t i) j", j=EG),
                                             AX.X, ALU.add))
                then(nc.vector.tensor_scalar(top[:].rearrange("p t e -> p (t e)"), rank[:], 1.5, None, ALU.is_lt))
                dve.wait_ge(eexp_done, i + 1)
                then(nc.vector.tensor_reduce(esum[:], eprob[:], AX.X, ALU.add))
                then(nc.vector.reciprocal(erec[:], esum[:]))
                then(nc.vector.tensor_tensor(pn[:], eprob[:], erec[:].unsqueeze(2).to_broadcast([P, TILES, EG]),
                                             ALU.mult))
                then(nc.vector.tensor_tensor(topp[:], pn[:], top[:], ALU.mult))
                then(nc.vector.tensor_reduce(tsum[:], topp[:], AX.X, ALU.add))
                nc.vector.tensor_tensor(cnt[:, :, 0:EXPERTS].rearrange("p t (g e) -> p t g e", e=EG),
                                        top[:].unsqueeze(2).to_broadcast([P, TILES, GROUPS, EG]), gmb, ALU.mult)
                then(nc.vector.tensor_scalar(tden[:], tsum[:], 1e-8, None, ALU.add))
                nc.vector.reciprocal(trec[:], tden[:]).then_inc(route_step, 1)
                dve.wait_ge(route_step, (i + 1) * ROUTE)

            def weights(i):
                nc.vector.tensor_tensor(wsel[:], topp[:], trec[:].unsqueeze(2).to_broadcast([P, TILES, EG]),
                                        ALU.mult).then_inc(wsel_made, 1)
                dve.wait_ge(wsel_made, 2 * i + 1)
                nc.vector.tensor_tensor(comb[:], wsel[:].unsqueeze(2).to_broadcast([P, TILES, GROUPS, EG]),
                                        gm[:].unsqueeze(3).to_broadcast([P, TILES, GROUPS, EG]),
                                        ALU.mult).then_inc(wsel_made, 1)

            def tail(i, st):
                kind = st[0]
                if kind == "route":
                    route(i)
                    weights(i)
                if kind == "in":
                    q = st[1]
                    ex, c, half = IN_STEPS[q]
                    ab = pair[q % 2]
                    dve.wait_ge(tanh_done, i * 8 + q + 1)
                    if later(i) or q:
                        dve.wait_ge(hid_made, i * 8 + q)
                    nc.vector.scalar_tensor_tensor(gate[:], th[:, q % 2, :], 1.0, ab[:, 0:HALF], ALU.add,
                                                   ALU.mult).then_inc(gate_made, 1)
                    dve.wait_ge(gate_made, i * 8 + q + 1)
                    nc.vector.scalar_tensor_tensor(hid[:, ex, c, halfs(half)], gate[:], 0.5, ab[:, HALF:2 * HALF],
                                                   ALU.mult, ALU.mult).then_inc(hid_made, 1)
                    if ex:
                        dve.wait_ge(hid_made, i * 8 + q + 1)
                        nc.vector.tensor_copy(hid_h[:, c, halfs(half)], hid[:, 1, c, halfs(half)]).then_inc(hidh_made, 1)
                if kind == "shared":
                    half = st[1]
                    dve.wait_ge(shared_ready, i * 2 + half + 1)
                    nc.vector.tensor_tensor(acc[:, tiles(half), :], (b4, b5)[half][:].rearrange("p (t c) -> p t c", c=P),
                                            h2[:, tiles(half), :], ALU.add).then_inc(base_made, 1)
                    dve.wait_ge(base_made, i * 2 + half + 1)
                if kind == "expert":
                    t = st[1]
                    dve.wait_ge(ex_ready, i * TILES + t + 1)
                    if t == 0:
                        dve.wait_ge(wsel_made, 2 * i + 2)
                    for e in range(EXPERTS):
                        n = t * EXPERTS + e
                        if e:
                            dve.wait_ge(ex_step, i * TILES * EXPERTS + n)
                        nc.vector.scalar_tensor_tensor(acc[:, t, :], pair[t % 2][:, e * P:(e + 1) * P],
                                                       comb[:, t, e // EG, e % EG:e % EG + 1], acc[:, t, :],
                                                       ALU.mult, ALU.add).then_inc(ex_step, 1)

            def image(i, another=True):
                attention(i)
                post(i)
                for st, nxt in woven_tail(another):
                    front(i + 1, st) if nxt else tail(i, st)

            dve.wait_ge(const_made, CONSTS)
            for st in FRONT:
                front(0, st)
            dve.wait_ge(w_in2, 9 * 16)
            image(0)
            with dve.Fori(1, B - 1) as i:
                image(i)
            image(B - 1, False)

        @block.scalar
        def _(act):
            def front(i, st):
                kind = st[0]
                if kind == "turn1":
                    half = st[1]
                    act.wait_ge(front_mm, i * 10 + 3 + half)
                    nc.scalar.copy(zt[:, halfs(half)], (b6, b7)[half][:]).then_inc(front_act, 1)
                if kind == "qk":
                    half = st[1]
                    for w, src, bias in ((0, b6, bq_sb), (1, b7, bk_sb)):
                        act.wait_ge(front_mm, i * 10 + 5 + 2 * half + w)
                        nc.scalar.activation(qk[:, w, halfs(half)], src[:], ACT.Identity,
                                             bias=bias[:, 0:1]).then_inc(front_act, 1)

            def attention(i):
                taken = 0

                def take(u):
                    g, half = UNITS[u]
                    last = max(k for k, (uu, _) in enumerate(PROB_STEPS) if uu == u)
                    act.wait_ge(pv_done, i * NP_ + last + 1)
                    nc.scalar.copy(ot[:, g, halfs(half)], b6[:]).then_inc(pv_taken, 1)

                for k, (u, kt) in enumerate(PROB_STEPS):
                    q0, _ = prob_columns(k)
                    if k >= PT_SLOTS:
                        act.wait_ge(pv_done, i * NP_ + k - 1)
                    elif later(i):
                        act.wait_ge(pv_done, i * NP_)
                    for j in range(G4):
                        p = k * G4 + j
                        act.wait_ge(st_ready, i * NP_ * G4 + p + 1)
                        nc.scalar.activation(pt[:, k % PT_SLOTS, j, q0:HALF], (b4, b5)[p % 2][:, q0:HALF], ACT.Exp,
                                             scale=0.25).then_inc(exp_done, 1)
                    if kt == 0 and u > 0:
                        take(u - 1)
                take(NU - 1)

            def post(i):
                for half, src in ((0, b4), (1, b5)):
                    act.wait_ge(ant_ready, i * 2 + half + 1)
                    nc.scalar.copy(ant[:, halfs(half)], src[:]).then_inc(ant_made, 1)
                for half, src in ((0, b4), (1, b5)):
                    act.wait_ge(z2t_ready, i * 2 + half + 1)
                    nc.scalar.activation(z2t[:, halfs(half)], src[:], ACT.Identity, bias=lnb_sb[:, 0:1],
                                         scale=lns_sb[:, 0:1]).then_inc(z2t_made, 1)

            def tail(i, st):
                kind = st[0]
                if kind == "route":
                    act.wait_ge(route_step, i * ROUTE + 7)
                    nc.scalar.activation(eprob[:], esub[:], ACT.Exp).then_inc(eexp_done, 1)
                if kind == "in":
                    q = st[1]
                    act.wait_ge(in_ready, i * 8 + q + 1)
                    nc.scalar.activation(th[:, q % 2, :], pair[q % 2][:, 0:HALF], ACT.Tanh,
                                         scale=0.5).then_inc(tanh_done, 1)
                if kind == "counts":
                    half = st[1]
                    act.wait_ge(cnt_ready, i * 2 + half + 1)
                    nc.scalar.copy(cnt_t[:, halfs(half)], b5[0:EXPERTS + 1, :]).then_inc(cnt_taken, 1)

            def image(i, another=True):
                attention(i)
                post(i)
                for st, nxt in woven_tail(another):
                    front(i + 1, st) if nxt else tail(i, st)

            act.wait_ge(w_in1, 9 * 16)
            for st in FRONT:
                front(0, st)
            act.wait_ge(w_in2, 9 * 16)
            nc.scalar.copy(win_h[:], win_sb).then_inc(wsplit_h, 1)
            nc.scalar.copy(wex_h[:], wex_sb).then_inc(wsplit_h, 1)
            image(0)
            with act.Fori(1, B - 1) as i:
                image(i)
            image(B - 1, False)

        @block.gpsimd
        def _(pool):
            zeroed = sem_zero
            nc.gpsimd.memset(ident[:], 0.0).then_inc(zeroed, 1)
            nc.gpsimd.memset(causal[:], 0.0).then_inc(zeroed, 1)
            nc.gpsimd.memset(tri[:], 1.0).then_inc(zeroed, 1)
            nc.gpsimd.memset(v[:], 0.0).then_inc(zeroed, 1)
            nc.gpsimd.memset(words(q_stack[:]), 0.0).then_inc(zeroed, 1)
            nc.gpsimd.memset(words(k_stack[:]), 0.0).then_inc(zeroed, 1)
            pool.wait_ge(zeroed, 6)
            nc.gpsimd.affine_select(out=ident[:], in_=ident[:], compare_op=ALU.not_equal, fill=1.0, base=0,
                                    pattern=[[-1, P]], channel_multiplier=1).then_inc(const_made, 1)
            nc.gpsimd.affine_select(out=causal[:, S - P:S], in_=causal[:, S - P:S], compare_op=ALU.is_ge, fill=MASK,
                                    base=0, pattern=[[-1, P]], channel_multiplier=1).then_inc(const_made, 1)
            nc.gpsimd.affine_select(out=tri[:].rearrange("p (i j) -> p i j", j=EG),
                                    in_=tri[:].rearrange("p (i j) -> p i j", j=EG), compare_op=ALU.is_gt, fill=0.0,
                                    base=0, pattern=[[1, EG], [-1, EG]], channel_multiplier=0).then_inc(const_made, 1)
            nc.gpsimd.memset(v[:, :, :, DH:DH + 1], 1.0).then_inc(const_made, 1)
            nc.gpsimd.memset(half_pow[:], -0.5).then_inc(const_made, 1)
            nc.gpsimd.memset(words(minus1[:]), -1.0).then_inc(const_made, 1)
            nc.gpsimd.memset(cnt[:, :, EXPERTS:EXPERTS + 1], 1.0).then_inc(const_made, 1)
            pool.wait_ge(const_made, CONSTS)
            pool.wait_ge(w_in1, 9 * 16)

            def front(i, st):
                kind = st[0]
                if kind == "emb":
                    alone(pool, mv_made, (i + 1) * TILES)
                    nc.gpsimd.tensor_scalar(var1[:], mv[:, :, 1], EPS, None, ALU.add).then_inc(var_made, 1)
                    pool.wait_ge(var_made, i + 1)
                    nc.gpsimd.tensor_tensor(rs1[:], var1[:], half_pow[:], ALU.pow).then_inc(rs_made, 1)
                    if later(i):
                        pool.wait_ge(h2_made, i * 2)
                    nc.gpsimd.tensor_tensor(hb[:], h[:], bo_sb[:].unsqueeze(1).to_broadcast([P, TILES, P]),
                                            ALU.add).then_inc(hb_made, 1)
                if kind == "turn1":
                    half = st[1]
                    pool.wait_ge(zth_made, i * 2 + half + 1)
                    nc.gpsimd.tensor_tensor(zt_l[:, halfs(half)], zt[:, halfs(half)], zt_h[:, halfs(half)].bitcast(F32),
                                            ALU.subtract).then_inc(ztl_made, 1)
                if kind == "qk":
                    half = st[1]
                    for w in range(2):
                        pool.wait_ge(qkh_made, i * 4 + 2 * half + w + 1)
                        nc.gpsimd.tensor_tensor(qk_l[:, w, halfs(half)], qk[:, w, halfs(half)],
                                                qk_h[:, w, halfs(half)].bitcast(F32), ALU.subtract).then_inc(qkl_made, 1)

            def attention(i):
                for n, k in enumerate(DIAG):
                    u, kt = PROB_STEPS[k]
                    q0, _ = prob_columns(k)
                    alone(pool, exp_done, i * NP_ * G4 + (k + 1) * G4)
                    d = pt[:, k % PT_SLOTS, :, q0:q0 + P]
                    nc.gpsimd.affine_select(out=d, in_=d, compare_op=ALU.is_ge, fill=0.0, base=0,
                                            pattern=[[0, G4], [1, P]], channel_multiplier=-1).then_inc(mask_done, 1)

            def post(i):
                def then(ins, n):
                    ins.then_inc(ln2_step, 1)
                    pool.wait_ge(ln2_step, i * 6 + n)

                alone(pool, mv2_made, (i + 1) * TILES)
                then(nc.gpsimd.tensor_scalar(t1[:], mv2[:, :, 1], EPS, None, ALU.add), 1)
                then(nc.gpsimd.tensor_tensor(t2[:], t1[:], half_pow[:], ALU.pow), 2)
                then(nc.gpsimd.tensor_tensor(t3[:], mv2[:, :, 1], t2[:], ALU.mult), 3)
                nc.gpsimd.tensor_tensor(t4[:], t3[:], t2[:], ALU.mult).then_inc(ln2_step, 1)
                alone(pool, ln2_step, i * 6 + 4)
                nc.gpsimd.tensor_scalar(t4e[:], t4[:], EPS, None, ALU.add).then_inc(ln2_mid, 1)
                pool.wait_ge(ln2_mid, i + 1)
                then(nc.gpsimd.tensor_tensor(t5[:], t4e[:], half_pow[:], ALU.pow), 5)
                then(nc.gpsimd.tensor_tensor(t6[:], t5[:], t2[:], ALU.mult), 6)
                for half in range(2):
                    pool.wait_ge(z2h_made, i * 2 + half + 1)
                    nc.gpsimd.tensor_tensor(z2t_l[:, halfs(half)], z2t[:, halfs(half)],
                                            z2t_h[:, halfs(half)].bitcast(F32), ALU.subtract).then_inc(z2l_made, 1)

            def tail(i, st):
                if st[0] == "in":
                    ex, c, half = IN_STEPS[st[1]]
                    if ex:
                        n = [q for q, s in enumerate(IN_STEPS) if s[0]].index(st[1])
                        pool.wait_ge(hidh_made, i * 4 + n + 1)
                        nc.gpsimd.tensor_tensor(hid_l[:, c, halfs(half)], hid[:, 1, c, halfs(half)],
                                                hid_h[:, c, halfs(half)].bitcast(F32), ALU.subtract).then_inc(hidl_made, 1)

            def image(i, another=True):
                attention(i)
                post(i)
                for st, nxt in woven_tail(another):
                    front(i + 1, st) if nxt else tail(i, st)

            for st in FRONT:
                front(0, st)
            pool.wait_ge(wsplit_h, 1)
            nc.gpsimd.tensor_tensor(win_l[:], win_sb, win_h[:].bitcast(F32), ALU.subtract).then_inc(wsplit_l, 1)
            pool.wait_ge(wsplit_h, 2)
            nc.gpsimd.tensor_tensor(wex_l[:], wex_sb, wex_h[:].bitcast(F32), ALU.subtract).then_inc(wsplit_l, 1)
            image(0)
            with pool.Fori(1, B - 1) as i:
                image(i)
            image(B - 1, False)


def position_table():
    import math
    position = np.arange(2 * S, dtype=np.float32)[:, None]
    div_term = np.exp(np.arange(0, P, 2, dtype=np.float32) * (-math.log(10000.0) / P))
    pe = np.zeros((2 * S, P), dtype=np.float32)
    pe[:, 0::2] = np.sin(position * div_term)
    pe[:, 1::2] = np.cos(position * div_term)
    return np.ascontiguousarray(pe[:S].reshape(TILES, P, P).transpose(1, 0, 2))


def kernel(**inputs):
    import numpy as _np
    import concourse.bacc as _bacc
    from concourse import mybir as _mybir
    from concourse.bass_utils import run_bass_kernel_spmd as _run

    a = {k: _np.asarray(w) for k, w in inputs.items()}

    def rows(w):
        return _np.broadcast_to(w[None, :], (P, w.shape[0]))

    def column(w):
        return w.reshape(P, 1)

    laid = {
        "x_t": a["x"].reshape(B * S, F).T,
        "tok_w": a["L0_tok_W"],
        "pos": position_table(),
        "wq": a["L0_attn_Wq"], "wk": a["L0_attn_Wk"], "wv": a["L0_attn_Wv"], "wo": a["L0_attn_Wo"],
        "bq": column(a["L0_attn_bq"]), "bk": column(a["L0_attn_bk"]),
        "bv": rows(a["L0_attn_bv"]), "bo": rows(a["L0_attn_bo"]),
        "ln_s": column(a["L0_ffn_ln_scale"]), "ln_b": column(a["L0_ffn_ln_bias"]),
        "w_in": _np.concatenate([a["L0_ffn_shared_in_w"], a["L0_ffn_expert_in_w"]], 0).T,
        "w_shared": a["L0_ffn_shared_out_w"].T.reshape(HID // P, P, P).transpose(1, 0, 2),
        "w_expert": a["L0_ffn_expert_out_weight"].transpose(2, 0, 1).reshape(HID // P, P, EXPERTS * P).transpose(1, 0, 2),
        "w_bias": _np.concatenate([a["L0_ffn_expert_out_bias"], a["L0_ffn_shared_out_b"][None, :]], 0),
        "w_gate": _np.concatenate([a["L0_ffn_group_gate_w"], a["L0_ffn_expert_gate_w"]], 0).T,
        "b_gate": rows(_np.concatenate([a["L0_ffn_group_bias"], a["L0_ffn_expert_bias"]])),
    }
    nc = _bacc.Bacc("TRN2", target_bir_lowering=False, num_devices=1)
    arrays, args = {}, []
    for name, w in laid.items():
        w = _np.ascontiguousarray(w)
        arrays[name] = w
        args.append(nc.dram_tensor(name, w.shape, _mybir.dt.from_np(w.dtype), kind="ExternalInput").ap())
    args.append(nc.dram_tensor("out", (B, S, P), _mybir.dt.float32, kind="ExternalOutput").ap())
    build(nc, *args)
    r = _run(nc, [arrays], core_ids=[0])
    return r.results[0]["out"]
```

```python
from contextlib import ExitStack

import numpy as np
import concourse.bass as bass
from concourse import mybir

F32 = mybir.dt.float32
F32R = mybir.dt.float32r
ALU = mybir.AluOpType
ACT = mybir.ActivationFunctionType
AX = mybir.AxisListType

P = 128
B, S, F = 8, 1024, 29
TILES = S // P
HALF = 512
HT = HALF // P
HEADS, DH = 8, 16
G4 = 4
HID = 256
EXPERTS, GROUPS, EG = 8, 2, 4
NGATE = GROUPS + EXPERTS
ODD = 64
STACK = ODD + 3 * DH
SHIFT = P - 2
EPS = 1e-5
MASK = -100000.0
VW = 32

UNITS = [(0, 0), (1, 0), (0, 1), (1, 1)]
SCORE_STEPS = [(u, HT * half + t, j) for u, (g, half) in enumerate(UNITS) for t in range(HT) for j in range(G4)]
PROB_STEPS = [(u, kt) for u, (g, half) in enumerate(UNITS) for kt in range(HT * (half + 1))]
NS, NP_, NU = len(SCORE_STEPS), len(PROB_STEPS), len(UNITS)
UNIT_S = NS // NU
DIAG = [k for k, (u, kt) in enumerate(PROB_STEPS) if kt >= HT * UNITS[u][1]]
UNIT_LAST = [max(k for k, (u, _) in enumerate(PROB_STEPS) if u == v) for v in range(NU)]
PT_SLOTS = 2


def prob_columns(k):
    u, kt = PROB_STEPS[k]
    q0 = max(0, kt * P - UNITS[u][1] * HALF)
    return q0, min(q0, HALF - 256)


def later(i):
    return not (isinstance(i, int) and i == 0)


IN_STEPS = [(kind, c, half) for half in range(2) for kind in (1, 0) for c in range(HID // P)]
NIN = len(IN_STEPS)
FRONT_STEPS = [("emb", 0), ("turn1", 0), ("q", 0), ("k", 0), ("emb", 1), ("v", 0), ("turn1", 1), ("q", 1), ("k", 1),
               ("v", 1)]
NF = len(FRONT_STEPS)
LN_STEPS = 7
ROUTE = 20


def of_next_image(st):
    return st[0] in ("emb", "turn1", "q", "k", "v") or st[0] == "score" and st[1] < 2 * UNIT_S or st[0] == "turn" and st[1] < 2


def streams():
    pass1 = []
    for u in (2, 3, 0, 1):
        pass1 += [("score", s) for s in range(u * UNIT_S, (u + 1) * UNIT_S)] + [("turn", u)]
    pass2 = []
    for k in range(NP_):
        pass2.append(("prob", k, 0))
        if k:
            pass2.append(("weigh", k - 1))
        pass2.append(("prob", k, 1))
        if k - 1 in UNIT_LAST:
            pass2.append(("take", UNIT_LAST.index(k - 1)))
    pass2 += [("weigh", NP_ - 1), ("take", NU - 1)]
    middle, forward = [], []
    for half in range(2):
        middle += [("to", half), ("ant", half), ("oproj", half), ("emb", half), ("z2t", half), ("gates", half),
                   ("route", half, 0)] + [("v", 0)] * half + [("turn1", half), ("route", half, 1), ("route", half, 2),
                   ("q", half), ("k", half)] + [("v", 1)] * half + [("counts", half), ("shared", half)]
        forward += [("in", q) for q in range(4 * half, 4 * half + 4)]
        forward += [("expert", t) for t in range(HT * half, HT * half + HT)]
    return {"s": pass1, "p": pass2, "m": middle, "f": forward}


WEAVE = (
    "ppsspspsspspspspspspspsppspssppsppsssppsspspspppspspspspppspppspppspsppsspppsmppppmppppppmpppmpp"
    "ppmppmpmpppmmpppmmpppmfppfffmppssmsssmssmsssmmffmsssmsmsfsfmsfsssssmssmfmssmfsmsmfmssmssfsffsf"
)


def period():
    left = {name: iter(stream) for name, stream in streams().items()}
    return [next(left[name]) for name in WEAVE]


PERIOD = period()
FIRST = [st for st in PERIOD if of_next_image(st)]
LAST = [st for st in PERIOD if not of_next_image(st)]


def build(nc, x_t, tok_w, pos, wq, wk, wv, wo, bq, bk, bv, bo, ln_s, ln_b, w_in, w_shared, w_expert, w_bias,
          w_gate, b_gate, out):
    with ExitStack() as ctx:
        def sb(name, shape, dt=F32):
            return ctx.enter_context(nc.sbuf_tensor(name, shape, dt))

        def sem(name):
            return ctx.enter_context(nc.semaphore(name))

        bank = [ctx.enter_context(nc.psum_tensor(f"bank{n}", [P, HALF], F32)) for n in (4, 5, 6, 7)]
        pair = [ctx.enter_context(nc.psum_tensor(f"pair{n}", [P, 2 * HALF], F32)) for n in range(2)]
        b4, b5, b6, b7 = bank

        ident = sb("ident", [P, P])
        causal = sb("causal", [P, S])
        tri = sb("tri", [P, EG * EG])
        half_pow = sb("half_pow", [P, TILES])
        pos_sb = sb("pos_sb", [P, TILES, P])
        tokw_sb = sb("tokw_sb", [F, P])
        wq_sb, wk_sb, wv_sb, wo_sb = (sb(n, [P, P]) for n in ("wq_sb", "wk_sb", "wv_sb", "wo_sb"))
        wqk_h = sb("wqk_h", [P, 2, P], F32R)
        wqk_l = sb("wqk_l", [P, 2, P], F32R)
        bq_sb, bk_sb, lns_sb, lnb_sb = (sb(n, [P, 1]) for n in ("bq_sb", "bk_sb", "lns_sb", "lnb_sb"))
        bv_sb, bo_sb = sb("bv_sb", [P, P]), sb("bo_sb", [P, P])
        bgate_sb = sb("bgate_sb", [P, NGATE])
        wgate_sb = sb("wgate_sb", [P, NGATE])
        wbias_sb = sb("wbias_sb", [EXPERTS + 1, P])
        wshared_sb = sb("wshared_sb", [P, HID // P, P])
        win_h, win_l = sb("win_h", [P, 4 * HID], F32R), sb("win_l", [P, 4 * HID], F32R)
        wex_h = sb("wex_h", [P, HID // P, EXPERTS * P], F32R)
        wex_l = sb("wex_l", [P, HID // P, EXPERTS * P], F32R)

        x_sb = sb("x_sb", [F, S])
        h = sb("h", [P, TILES, P])
        stats = sb("stats", [P, TILES, 6])
        mv = sb("mv", [P, TILES, 2])
        var1 = sb("var1", [P, TILES])
        rs1 = sb("rs1", [P, TILES])
        z = sb("z", [P, TILES, P])
        zt = sb("zt", [P, S])
        zt_h, zt_l = sb("zt_h", [P, S], F32R), sb("zt_l", [P, S], F32R)
        qk_h, qk_l = sb("qk_h", [P, 2, S], F32R), sb("qk_l", [P, 2, S], F32R)
        v = sb("v", [P, TILES, HEADS, VW])
        q_stack = sb("q_stack", [P, 2, HEADS, HALF], F32R)
        k_stack = sb("k_stack", [P, HEADS // 2, S], F32R)
        mx = sb("mx", [P, NS])
        mrow_h, mrow_l = sb("mrow_h", [UNIT_S, NU, P], F32R), sb("mrow_l", [UNIT_S, NU, P], F32R)
        pt = sb("pt", [P, PT_SLOTS, G4, HALF])
        wex_sb = pt[:, 0, :, :].rearrange("p (c x) q -> p c (x q)", c=HID // P)
        win_sb = pt[:, 1, 0:2, :].rearrange("p x q -> p (x q)")
        ot = sb("ot", [P, 2, S])
        qk = ot
        rec = sb("rec", [P, TILES, HEADS])
        an, ant = z, zt
        h2 = sb("h2", [P, TILES, P])
        stats2 = sb("stats2", [P, TILES, 6])
        mv2 = sb("mv2", [P, TILES, 2])
        t1, t2, t3, t4, t5, t6 = (sb(f"ln_{n}", [P, TILES]) for n in range(6))
        t4e = sb("ln_4e", [P, TILES])
        z2, z2t = z, zt
        z2t_h, z2t_l = sb("z2t_h", [P, S], F32R), sb("z2t_l", [P, S], F32R)
        gl = sb("gl", [P, TILES, NGATE])
        gm = sb("gm", [P, TILES, GROUPS])
        both = sb("both", [P, TILES, GROUPS, EG])
        esel = sb("esel", [P, TILES, EG])
        emax = sb("emax", [P, TILES])
        esub = sb("esub", [P, TILES, EG])
        eprob = sb("eprob", [P, TILES, EG])
        esum = sb("esum", [P, TILES])
        cmp_gt, cmp_eq = sb("cmp_gt", [P, TILES, EG * EG]), sb("cmp_eq", [P, TILES, EG * EG])
        cmp_tie, cmp_all = sb("cmp_tie", [P, TILES, EG * EG]), sb("cmp_all", [P, TILES, EG * EG])
        rank = sb("rank", [P, TILES, EG])
        top = sb("top", [P, TILES, EG])
        topp = sb("topp", [P, TILES, EG])
        tsum, tden, trec = sb("tsum", [P, TILES]), sb("tden", [P, TILES]), sb("trec", [P, TILES])
        wsel = sb("wsel", [P, TILES, EG])
        cnt = sb("cnt", [P, TILES, EXPERTS + 1])
        cnt_t = sb("cnt_t", [EXPERTS + 1, HALF])
        from_act = sb("from_act", [P, 2, HALF])
        from_dve = sb("from_dve", [P, 2, HALF])
        hid = sb("hid", [P, 2, HID // P, HALF])
        hid_h = sb("hid_h", [P, HID // P, HALF], F32R)
        hid_l = sb("hid_l", [P, HID // P, HALF], F32R)
        minus1 = hid_l[0:2, :, :]
        acc = h2

        w_in1 = sem("w_front_loaded")
        w_in2 = sem("w_rest_loaded")
        const_made = sem("const_made")
        ones_in = sem("minus_ones_in_stack")
        wsplit_qk = sem("wsplit_qk")
        wsplit_h = sem("wsplit_h")
        wsplit_l = sem("wsplit_l")
        x_in = sem("x_in")
        front_mm = sem("front_mm")
        h_made = sem("h_made")
        zt_made, qk_made = sem("zt_made"), sem("qk_made")
        hb_made = sem("hb_made")
        stat1 = sem("stat1")
        mv_made = sem("mv_made")
        var_made = sem("var_made")
        rs_made = sem("rs_made")
        z_made = sem("z_made")
        zth_made, ztl_made = sem("zth_made"), sem("ztl_made")
        qkh_made, qkl_made = sem("qkh_made"), sem("qkl_made")
        v_made = sem("v_made")
        stack_in = [sem(f"stack_in_{half}") for half in range(2)]
        s_ready, s_taken = sem("scores_ready"), sem("scores_taken")
        m_turned, mh_made, ml_made, m_in = sem("max_turned"), sem("mh_made"), sem("ml_made"), [sem(f"max_in_stack_{u}") for u in range(NU)]
        st_ready, exp_done, mask_done = sem("st_ready"), sem("exp_done"), sem("mask_done")
        pv_done, pv_taken = sem("pv_done"), sem("pv_taken")
        to_ready, rec_made, an_made = sem("to_ready"), sem("rec_made"), sem("an_made")
        ant_ready, ant_made = sem("ant_ready"), sem("ant_made")
        o_ready, h2_made = sem("o_ready"), sem("h2_made")
        stat2, mv2_made, ln2_step, z2_made = sem("stat2"), sem("mv2_made"), sem("ln2_step"), sem("z2_made")
        z2t_ready, z2t_made = sem("z2t_ready"), sem("z2t_made")
        z2h_made, z2l_made = sem("z2h_made"), sem("z2l_made")
        gl_ready, route_step, eexp_done = sem("gl_ready"), sem("route_step"), sem("eexp_done")
        in_ready, tanh_done, gate_made, hid_made = sem("in_ready"), sem("tanh_done"), sem("gate_made"), sem("hid_made")
        hidh_made, hidl_made = sem("hidh_made"), sem("hidl_made")
        cnt_ready, cnt_taken = sem("cnt_ready"), sem("cnt_taken")
        shared_ready, base_made = sem("shared_ready"), sem("base_made")
        ex_ready, sela_made, sel_made, ex_step = (sem(n) for n in ("ex_ready", "sela_made", "sel_made", "ex_step"))
        out_done = [sem(f"out_done_{half}") for half in range(2)]
        sem_zero = sem("sem_zero")
        went_on = sem("went_on")

        out_v = out.rearrange("b (t p) c -> b p t c", p=P)
        CONSTS = 7

        def halfs(half):
            return slice(half * HALF, (half + 1) * HALF)

        def tiles(half):
            return slice(half * HT, (half + 1) * HT)

        def front_step(i, what, half):
            return i * NF + FRONT_STEPS.index((what, half)) + 1

        def words(ap):
            return ap.bitcast(F32)

        def alone(eng, semaphore, value):
            eng.wait_ge(semaphore, value)
            eng.sem_inc(went_on, 1)

        block = ctx.enter_context(nc.Block())

        @block.sync
        def _(sp):
            def load_x(i):
                sp.dma_start(x_sb[:], x_t[:, bass.ds(i * S, S)]).then_inc(x_in, 16)

            load_x(0)
            for dst, src in ((tokw_sb, tok_w), (pos_sb, pos), (wq_sb, wq), (wk_sb, wk), (bq_sb, bq), (bk_sb, bk),
                             (wv_sb, wv), (bv_sb, bv), (bo_sb, bo)):
                sp.dma_start(dst[:], src).then_inc(w_in1, 16)
            for dst, src in ((wo_sb, wo), (lns_sb, ln_s), (lnb_sb, ln_b), (win_sb, w_in), (wshared_sb, w_shared),
                             (wex_sb, w_expert), (wbias_sb, w_bias), (wgate_sb, w_gate), (bgate_sb, b_gate)):
                sp.dma_start(dst if dst is win_sb or dst is wex_sb else dst[:], src).then_inc(w_in2, 16)
            sp.wait_ge(const_made, CONSTS)
            for n in range(HEADS // 2):
                sp.dma_start(words(k_stack[SHIFT:P, n, :]), words(minus1.rearrange("r c n -> r (c n)"))).then_inc(ones_in, 16)

            def stacks(i, half, w):
                if w == 0:
                    sp.wait_ge(qkh_made, i * 4 + 2 * half + 2)
                    sp.wait_ge(qkl_made, i * 4 + 2 * half + 2)
                for n, part in enumerate((qk_h, (qk_h, qk_l)[w], (qk_l, qk_h)[w])):
                    for odd in range(2):
                        to = slice(odd * ODD + n * DH, odd * ODD + (n + 1) * DH)
                        stack = k_stack[to, :, halfs(half)] if w else q_stack[to, half, odd::2, :]
                        rows = part[odd * (P // 2):(odd + 1) * (P // 2), w, halfs(half)]
                        sp.dma_start(words(stack), words(rows)).then_inc(stack_in[half], 16)

            def maxima(i, u):
                g, half = UNITS[u]
                sp.wait_ge(ml_made, i * NU + u + 1)
                for row, part in ((SHIFT, mrow_h), (SHIFT + 1, mrow_l)):
                    dst = q_stack[row:row + 1, half, g * G4:(g + 1) * G4, :]
                    sp.dma_start(words(dst), words(part[:, u, :])).then_inc(m_in[u], 16)

            def store(i, half):
                sp.wait_ge(ex_step, (i * TILES + (half + 1) * HT) * EG)
                sp.dma_start(out_v[i, :, tiles(half), :], acc[:, tiles(half), :]).then_inc(out_done[half], 16)

            def stage(i, st, loads=True):
                if st[0] == "turn":
                    maxima(i, st[1])
                elif st == ("k", 0):
                    stacks(i, 0, 0)
                    if not later(i):
                        stacks(i, 0, 1)
                elif st == ("k", 1):
                    stacks(i, 1, 0)
                    stacks(i, 1, 1)
                    if loads:
                        load_x(i + 1)
                elif st == ("expert", 3):
                    store(i, 0)
                elif st == ("expert", 7):
                    store(i, 1)

            def keys(i):
                sp.wait_ge(exp_done, (i + 1) * NP_ * G4)
                stacks(i + 1, 0, 1)

            def image(i, loads):
                for st in PERIOD:
                    if st == ("take", NU - 1):
                        keys(i)
                    stage(i + of_next_image(st), st, loads)

            for st in FIRST:
                stage(0, st)
            image(0, True)
            with sp.Fori(1, B - 2) as i:
                image(i, True)
            image(B - 2, False)
            for st in LAST:
                stage(B - 1, st)
            for half in range(2):
                sp.wait_ge(out_done[half], B * 16)

        @block.tensor
        def _(pe):
            def split_mm(dst, wh, wl, xh, xl, first=True, last=True):
                nc.tensor.matmul(dst, wh, xh, start=first, stop=False)
                nc.tensor.matmul(dst, wl, xh, start=False, stop=False)
                return nc.tensor.matmul(dst, wh, xl, start=False, stop=last)

            def front(i, kind, half):
                if kind == "emb":
                    pe.wait_ge(x_in, (i + 1) * 16)
                    if later(i) and half == 0:
                        pe.wait_ge(ml_made, i * NU)
                    if later(i) and half == 1:
                        pe.wait_ge(ant_made, i * 2)
                    for t in range(HT):
                        mm = nc.tensor.matmul((b7, b6)[half][:, t * P:(t + 1) * P],
                                              x_sb[:, (half * HT + t) * P:(half * HT + t + 1) * P],
                                              tokw_sb[:], start=True, stop=True)
                    mm.then_inc(front_mm, 1)
                if kind == "turn1":
                    pe.wait_ge(z_made, i * TILES + (half + 1) * HT)
                    if later(i) and half == 1:
                        pe.wait_ge(z2h_made, i * 2)
                    for t in range(HT):
                        mm = nc.tensor.transpose((b7, b6)[half][:, t * P:(t + 1) * P], z[:, half * HT + t, :], ident[:])
                    mm.then_inc(front_mm, 1)
                if kind in ("q", "k"):
                    w = "qk".index(kind)
                    pe.wait_ge(ztl_made, i * 2 + half + 1)
                    pe.wait_ge(zth_made, i * 2 + half + 1)
                    if w == 0 and half:
                        pe.wait_ge(v_made, i * 2 + 1)
                    if w and half == 0:
                        pe.wait_ge(qkh_made, i * 4 + 1)
                    split_mm((b6 if half and w else b7)[:], wqk_h[:, w, :], wqk_l[:, w, :], zt_h[:, halfs(half)],
                             zt_l[:, halfs(half)]).then_inc(front_mm, 1)
                if kind == "v":
                    if half:
                        pe.wait_ge(qkh_made, i * 4 + 3)
                    elif later(i):
                        pe.wait_ge(route_step, (i * 2 - 1) * ROUTE + 1)
                    else:
                        pe.wait_ge(qkh_made, i * 4 + 2)
                    for t in range(HT):
                        mm = nc.tensor.matmul(b7[:, t * P:(t + 1) * P],
                                              zt[:, (half * HT + t) * P:(half * HT + t + 1) * P],
                                              wv_sb[:], start=True, stop=True)
                    mm.then_inc(front_mm, 1)

            def score(i, s):
                u, t, j = SCORE_STEPS[s]
                hd = UNITS[u][0] * G4 + j
                if s == 0:
                    pe.wait_ge(stack_in[0], i * 192 + 192)
                    if later(i):
                        pe.wait_ge(exp_done, i * NP_ * G4)
                if s == UNIT_S:
                    pe.wait_ge(ml_made, i * NU + 1)
                if s == 2 * UNIT_S:
                    pe.wait_ge(stack_in[1], i * 192 + 192)
                    if later(i):
                        pe.wait_ge(sel_made, i * TILES)
                if s >= 2:
                    pe.wait_ge(s_taken, i * NS + s - 1)
                n = (t + 1) * P
                dst = pair[s % 2] if t >= HT else (b4, b5)[s % 2]
                for a, b in ([(0, max(256, n))] if n <= HALF else [(0, HALF), (HALF, max(HALF + 256, n))]):
                    mm = nc.tensor.matmul(dst[:, a:b], q_stack[0:STACK, t // HT, hd, t % HT * P:(t % HT + 1) * P],
                                          k_stack[0:STACK, hd // 2, a:b], start=True, stop=True)
                mm.then_inc(s_ready, 1)

            def turn(i, u):
                if u == 2 and later(i):
                    pe.wait_ge(cnt_taken, i * 2)
                if u == 2:
                    pe.wait_ge(v_made, i * 2 + 2)
                if u == 3:
                    pe.wait_ge(ml_made, i * NU + 3)
                pe.wait_ge(s_taken, i * NS + (u + 1) * UNIT_S)
                nc.tensor.transpose((b4 if u < 2 else b7)[0:UNIT_S, 0:P], mx[:, u * UNIT_S:(u + 1) * UNIT_S],
                                    ident[:]).then_inc(m_turned, 1)

            def prob(i, k, part):
                u, kt = PROB_STEPS[k]
                g, half = UNITS[u]
                q0, c0 = prob_columns(k)
                if kt == 0 and part == 0:
                    pe.wait_ge(m_in[u], i * 32 + 32)
                if k == 0 and part == 0:
                    pe.wait_ge(ml_made, i * NU + 2)
                for j in (2 * part, 2 * part + 1):
                    p = k * G4 + j
                    if p >= 2:
                        pe.wait_ge(exp_done, i * NP_ * G4 + p - 1)
                    hd = g * G4 + j
                    nc.tensor.matmul((b4, b5)[p % 2][:, c0:HALF], k_stack[:, hd // 2, kt * P:(kt + 1) * P],
                                     q_stack[:, half, hd, c0:HALF],
                                     start=True, stop=True).then_inc(st_ready, 1)

            def weigh(i, k):
                u, kt = PROB_STEPS[k]
                g, half = UNITS[u]
                q0, _ = prob_columns(k)
                pe.wait_ge(exp_done, i * NP_ * G4 + (k + 1) * G4)
                if k in DIAG:
                    pe.wait_ge(mask_done, i * len(DIAG) + DIAG.index(k) + 1)
                if kt == 0 and u == 0:
                    pe.wait_ge(v_made, i * 2 + 2)
                    pe.wait_ge(qkh_made, i * 4 + 4)
                    if later(i):
                        pe.wait_ge(base_made, i * 2)
                if kt == 0 and u > 0:
                    pe.wait_ge(pv_taken, i * NU + u)
                for j in range(G4):
                    mm = nc.tensor.matmul(b6[32 * j:32 * j + VW, q0:HALF], v[:, kt, g * G4 + j, :],
                                          pt[:, k % PT_SLOTS, j, q0:HALF], start=(kt == 0),
                                          stop=(kt == HT * (half + 1) - 1), tile_position=(0, 32 * j))
                mm.then_inc(pv_done, 1)

            def post(i, st, more):
                kind, half = st[0], st[1]
                if kind == "to":
                    pe.wait_ge(pv_taken, i * NU + 2 * half + 2)
                    if half == 0:
                        pe.wait_ge(s_taken, (i + 1) * NS)
                    else:
                        pe.wait_ge(base_made, i * 2 + 1)
                    for n in range(2):
                        for m in range(2):
                            t = half * HT + 2 * n + m
                            for g in range(2):
                                to = m * 256 + g * P
                                dst = (b6, b7)[n][:, to:to + P] if half else pair[0][:, n * HALF + to:n * HALF + to + P]
                                mm = nc.tensor.transpose(dst, ot[:, g, t * P:(t + 1) * P], ident[:])
                        mm.then_inc(to_ready, 1)
                if kind == "ant":
                    pe.wait_ge(an_made, i * HT + 2 * half + 2)
                    for t in range(HT):
                        mm = nc.tensor.transpose((b6 if half else pair[1])[:, t * P:(t + 1) * P],
                                                 an[:, half * HT + t, :], ident[:])
                    mm.then_inc(ant_ready, 1)
                if kind == "oproj":
                    pe.wait_ge(ant_made, i * 2 + half + 1)
                    for t in range(HT):
                        tt = half * HT + t
                        dst = b7[:, t * P:(t + 1) * P] if half else pair[1][:, HALF + t * P:HALF + (t + 1) * P]
                        mm = nc.tensor.matmul(dst, ant[:, tt * P:(tt + 1) * P], wo_sb[:], start=True, stop=True)
                    mm.then_inc(o_ready, 1)
                if kind == "z2t":
                    pe.wait_ge(z2_made, i * TILES + (half + 1) * HT)
                    if half and more:
                        pe.wait_ge(h_made, (i + 1) * 2 + 2)
                    for t in range(HT):
                        mm = nc.tensor.transpose((b6 if half else pair[0])[:, t * P:(t + 1) * P],
                                                 z2[:, half * HT + t, :], ident[:])
                    mm.then_inc(z2t_ready, 1)
                if kind == "gates":
                    pe.wait_ge(z2t_made, i * 2 + half + 1)
                    for t in range(HT):
                        tt = half * HT + t
                        to = (0 if half else HALF) + t * NGATE
                        mm = nc.tensor.matmul((b7 if half else pair[0])[:, to:to + NGATE],
                                              z2t[:, tt * P:(tt + 1) * P], wgate_sb[:], start=True, stop=True)
                    mm.then_inc(gl_ready, 1)

            def forward(i, st, more):
                kind = st[0]
                if kind == "in":
                    q = st[1]
                    ex, c, half = IN_STEPS[q]
                    ab_pair = pair[q % 2]
                    if q % 4 == 0:
                        pe.wait_ge(z2h_made, i * 2 + half + 1)
                        pe.wait_ge(z2l_made, i * 2 + half + 1)
                    if q == 0:
                        pe.wait_ge(route_step, i * 2 * ROUTE + 1)
                    elif q == 1:
                        pe.wait_ge(h2_made, i * 2 + 1)
                    elif q % 4 < 2:
                        pe.wait_ge(sel_made, i * TILES + q - 1)
                    else:
                        pe.wait_ge(hid_made, i * NIN + q - 1)
                    for ab in range(2):
                        w0 = ex * 2 * HID + ab * HID + c * P
                        mm = split_mm(ab_pair[:, ab * HALF:(ab + 1) * HALF], win_h[:, w0:w0 + P],
                                      win_l[:, w0:w0 + P], z2t_h[:, halfs(half)], z2t_l[:, halfs(half)])
                    mm.then_inc(in_ready, 1)
                elif kind == "counts":
                    half = st[1]
                    pe.wait_ge(route_step, (i * 2 + half + 1) * ROUTE)
                    if half == 0 and more:
                        pe.wait_ge(qkh_made, (i + 1) * 4 + 2)
                    elif half == 0:
                        pe.wait_ge(ml_made, (i + 1) * NU)
                    elif more:
                        pe.wait_ge(v_made, (i + 1) * 2 + 2)
                    for t in range(HT):
                        mm = nc.tensor.transpose(b7[0:EXPERTS + 1, t * P:(t + 1) * P], cnt[:, half * HT + t, :], ident[:])
                    mm.then_inc(cnt_ready, 1)
                elif kind == "shared":
                    half = st[1]
                    pe.wait_ge(hid_made, i * NIN + (half + 1) * 4)
                    pe.wait_ge(cnt_taken, i * 2 + half + 1)
                    if half and more:
                        pe.wait_ge(qkh_made, (i + 1) * 4 + 4)
                    elif half:
                        pe.wait_ge(z2h_made, i * 2 + 2)
                    for t in range(HT):
                        dst = (b7, b6)[half][:, t * P:(t + 1) * P]
                        tok = slice(t * P, (t + 1) * P)
                        for c in range(HID // P):
                            nc.tensor.matmul(dst, hid[:, 0, c, tok], wshared_sb[:, c, :], start=(c == 0), stop=False)
                        mm = nc.tensor.matmul(dst, cnt_t[:, tok], wbias_sb[:], start=False, stop=True)
                    mm.then_inc(shared_ready, 1)
                elif kind == "expert":
                    t = st[1]
                    dst_pair = pair[t % 2]
                    if t % HT == 0:
                        pe.wait_ge(hidl_made, i * 4 + (t // HT + 1) * 2)
                        pe.wait_ge(hidh_made, i * 4 + (t // HT + 1) * 2)
                    if t % HT < 2:
                        pe.wait_ge(hid_made, i * NIN + t + 3)
                    else:
                        pe.wait_ge(sel_made, i * TILES + t - 1)
                    tok = slice(t % HT * P, (t % HT + 1) * P)
                    for g in range(GROUPS):
                        dst = dst_pair[:, g * HALF:(g + 1) * HALF]
                        w = slice(g * HALF, (g + 1) * HALF)
                        for c in range(HID // P):
                            nc.tensor.matmul(dst, hid_h[:, c, tok], wex_h[:, c, w], start=(c == 0), stop=False)
                            nc.tensor.matmul(dst, hid_h[:, c, tok], wex_l[:, c, w], start=False, stop=False)
                            mm = nc.tensor.matmul(dst, hid_l[:, c, tok], wex_h[:, c, w], start=False,
                                                  stop=(c == HID // P - 1))
                    mm.then_inc(ex_ready, 1)

            def stage(i, st, more=True):
                if st[0] == "score":
                    score(i, st[1])
                elif st[0] == "turn":
                    turn(i, st[1])
                elif st[0] == "prob":
                    prob(i, st[1], st[2])
                elif st[0] == "weigh":
                    weigh(i, st[1])
                elif of_next_image(st):
                    front(i, st[0], st[1])
                elif st[0] in ("in", "counts", "shared", "expert"):
                    forward(i, st, more)
                else:
                    post(i, st, more)

            def image(i):
                for st in PERIOD:
                    stage(i + of_next_image(st), st)

            pe.wait_ge(w_in1, 9 * 16)
            pe.wait_ge(const_made, CONSTS)
            pe.wait_ge(wsplit_qk, 4)
            for st in FIRST:
                stage(0, st)
            pe.wait_ge(ones_in, HEADS // 2 * 16)
            pe.wait_ge(w_in2, 9 * 16)
            pe.wait_ge(wsplit_h, 2)
            pe.wait_ge(wsplit_l, 2)
            image(0)
            with pe.Fori(1, B - 1) as i:
                image(i)
            for st in LAST:
                stage(B - 1, st, False)

        @block.vector
        def _(dve):
            dve.wait_ge(w_in1, 9 * 16)
            for n, w in enumerate((wq_sb, wk_sb)):
                nc.vector.tensor_copy(wqk_h[:, n, :], w[:]).then_inc(wsplit_qk, 1)
            dve.wait_ge(wsplit_qk, 2)
            for n, w in enumerate((wq_sb, wk_sb)):
                nc.vector.tensor_tensor(wqk_l[:, n, :], w[:], wqk_h[:, n, :].bitcast(F32),
                                        ALU.subtract).then_inc(wsplit_qk, 1)

            def front(i, kind, half):
                if kind == "emb":
                    dve.wait_ge(front_mm, front_step(i, "emb", half))
                    nc.vector.tensor_tensor(h[:, tiles(half), :], (b7, b6)[half][:].rearrange("p (t c) -> p t c", c=P),
                                            pos_sb[:, tiles(half), :], ALU.add).then_inc(h_made, 1)
                    dve.wait_ge(h_made, i * 2 + half + 1)
                    for t in range(half * HT, (half + 1) * HT):
                        nc.vector.bn_stats(stats[:, t, :], h[:, t, :]).then_inc(stat1, 1)
                    alone(dve, stat1, i * TILES + (half + 1) * HT)
                    for t in range(half * HT, (half + 1) * HT):
                        nc.vector.bn_aggr(mv[:, t, :], stats[:, t, :]).then_inc(mv_made, 1)
                if kind == "turn1":
                    dve.wait_ge(rs_made, i * 2 + half + 1)
                    for t in range(half * HT, (half + 1) * HT):
                        nc.vector.tensor_scalar(z[:, t, :], h[:, t, :], mv[:, t, 0:1], rs1[:, t:t + 1],
                                                ALU.subtract, ALU.mult).then_inc(z_made, 1)
                if kind == "k":
                    dve.wait_ge(z_made, i * TILES + (half + 1) * HT)
                    nc.vector.tensor_tensor(h[:, tiles(half), :], h[:, tiles(half), :],
                                            bo_sb[:].unsqueeze(1).to_broadcast([P, HT, P]), ALU.add).then_inc(hb_made, 1)
                if kind == "v":
                    dve.wait_ge(front_mm, front_step(i, "v", half))
                    bias = bv_sb[:].rearrange("p (h d) -> p h d", d=DH).unsqueeze(1)
                    nc.vector.tensor_tensor(v[:, tiles(half), :, 0:DH],
                                            b7[:].rearrange("p (t h d) -> p t h d", h=HEADS, d=DH),
                                            bias.to_broadcast([P, HT, HEADS, DH]), ALU.add).then_inc(v_made, 1)

            def maxima_split(i, u):
                dve.wait_ge(m_turned, i * NU + u + 1)
                src = (b4 if u < 2 else b7)[0:UNIT_S, 0:P]
                nc.vector.tensor_copy(mrow_h[:, u, :], src).then_inc(mh_made, 1)
                dve.wait_ge(mh_made, i * NU + u + 1)
                nc.vector.tensor_tensor(mrow_l[:, u, :], src, mrow_h[:, u, :].bitcast(F32),
                                        ALU.subtract).then_inc(ml_made, 1)

            def score(i, s):
                u, t, j = SCORE_STEPS[s]
                n = (t + 1) * P
                col = u * UNIT_S + j * HT + t % HT
                alone(dve, s_ready, i * NS + s + 1)
                src = (pair[s % 2] if t >= HT else (b4, b5)[s % 2])[:, 0:n]
                nc.vector.tensor_tensor_reduce(src, src, causal[:, S - n:S], 1.0, -3.0e38, ALU.add, ALU.max,
                                               mx[:, col:col + 1]).then_inc(s_taken, 1)

            def post(i, st):
                kind, half = st[0], st[1]
                if kind == "to":
                    for m in range(2):
                        n = 2 * half + m
                        dve.wait_ge(to_ready, i * HT + n + 1)
                        src = ((b6, b7)[m][:] if half else pair[0][:, m * HALF:(m + 1) * HALF]).rearrange(
                            "p (k w) -> p k w", w=VW)
                        rc = rec[:, 2 * n:2 * n + 2, :].rearrange("p t h -> p (t h)")
                        nc.vector.reciprocal(rc, src[:, :, DH]).then_inc(rec_made, 1)
                        dve.wait_ge(rec_made, i * HT + n + 1)
                        nc.vector.tensor_tensor(an[:, 2 * n:2 * n + 2, :].rearrange("p t (h d) -> p (t h) d", d=DH),
                                                src[:, :, 0:DH], rc.unsqueeze(2).to_broadcast([P, 2 * HEADS, DH]),
                                                ALU.mult).then_inc(an_made, 1)
                if kind == "oproj":
                    dve.wait_ge(hb_made, i * 2 + half + 1)
                    if later(i):
                        dve.wait_ge(out_done[half], i * 16)
                    src = b7[:] if half else pair[1][:, HALF:2 * HALF]
                    dve.wait_ge(o_ready, i * 2 + half + 1)
                    nc.vector.tensor_tensor(h2[:, tiles(half), :], src.rearrange("p (t c) -> p t c", c=P),
                                            h[:, tiles(half), :], ALU.add).then_inc(h2_made, 1)
                    dve.wait_ge(h2_made, i * 2 + half + 1)
                    for t in range(half * HT, (half + 1) * HT):
                        nc.vector.bn_stats(stats2[:, t, :], h2[:, t, :]).then_inc(stat2, 1)
                    alone(dve, stat2, i * TILES + (half + 1) * HT)
                    for t in range(half * HT, (half + 1) * HT):
                        nc.vector.bn_aggr(mv2[:, t, :], stats2[:, t, :]).then_inc(mv2_made, 1)
                if kind == "z2t":
                    dve.wait_ge(ln2_step, (i * 2 + half + 1) * LN_STEPS)
                    for t in range(half * HT, (half + 1) * HT):
                        nc.vector.tensor_scalar(z2[:, t, :], h2[:, t, :], mv2[:, t, 0:1], t6[:, t:t + 1],
                                                ALU.subtract, ALU.mult).then_inc(z2_made, 1)
                if kind == "route":
                    route(i, half, st[2])

            def route(i, half, part):
                base = (i * 2 + half) * ROUTE
                T = tiles(half)

                def needs(n):
                    dve.wait_ge(route_step, base + n)

                def step(ins):
                    ins.then_inc(route_step, 1)

                def over_i(ap):
                    return ap.unsqueeze(2).to_broadcast([P, HT, EG, EG])

                def over_j(ap):
                    return ap.unsqueeze(3).to_broadcast([P, HT, EG, EG])

                def square(ap):
                    return ap[:, T, :].rearrange("p t (i j) -> p t i j", j=EG)

                gmb = gm[:, T, :].unsqueeze(3).to_broadcast([P, HT, GROUPS, EG])
                if part == 0:
                    dve.wait_ge(gl_ready, i * 2 + half + 1)
                    src = (b7[:, 0:HT * NGATE] if half else pair[0][:, HALF:HALF + HT * NGATE])
                    step(nc.vector.tensor_tensor(gl[:, T, :], src.rearrange("p (t n) -> p t n", n=NGATE),
                                                 bgate_sb[:].unsqueeze(1).to_broadcast([P, HT, NGATE]), ALU.add))
                    needs(1)
                    step(nc.vector.tensor_tensor(gm[:, T, 0:1], gl[:, T, 1:2], gl[:, T, 0:1], ALU.is_le))
                    step(nc.vector.tensor_tensor(gm[:, T, 1:2], gl[:, T, 1:2], gl[:, T, 0:1], ALU.is_gt))
                    needs(3)
                    step(nc.vector.tensor_tensor(both[:, T, :, :], gl[:, T, GROUPS:].rearrange("p t (g e) -> p t g e", e=EG),
                                                 gmb, ALU.mult))
                    needs(4)
                    step(nc.vector.tensor_tensor(esel[:, T, :], both[:, T, 0, :], both[:, T, 1, :], ALU.add))
                    needs(5)
                    step(nc.vector.tensor_reduce(emax[:, T], esel[:, T, :], AX.X, ALU.max))
                    step(nc.vector.tensor_tensor(square(cmp_gt), over_i(esel[:, T, :]), over_j(esel[:, T, :]), ALU.is_gt))
                    step(nc.vector.tensor_tensor(square(cmp_eq), over_i(esel[:, T, :]), over_j(esel[:, T, :]), ALU.is_equal))
                    needs(6)
                    step(nc.vector.tensor_tensor(esub[:, T, :], esel[:, T, :], emax[:, T].unsqueeze(2).to_broadcast(
                        [P, HT, EG]), ALU.subtract))
                if part == 1:
                    needs(9)
                    step(nc.vector.tensor_tensor(cmp_tie[:, T, :], cmp_eq[:, T, :], tri[:].unsqueeze(1).to_broadcast(
                        [P, HT, EG * EG]), ALU.mult))
                    needs(10)
                    step(nc.vector.tensor_tensor(cmp_all[:, T, :], cmp_gt[:, T, :], cmp_tie[:, T, :], ALU.add))
                    needs(11)
                    step(nc.vector.tensor_reduce(rank[:, T, :], square(cmp_all), AX.X, ALU.add))
                    needs(12)
                    step(nc.vector.tensor_scalar(top[:, T, :], rank[:, T, :], 1.5, None, ALU.is_lt))
                    needs(13)
                    step(nc.vector.tensor_tensor(cnt[:, T, 0:EXPERTS].rearrange("p t (g e) -> p t g e", e=EG),
                                                 top[:, T, :].unsqueeze(2).to_broadcast([P, HT, GROUPS, EG]), gmb, ALU.mult))
                if part == 2:
                    needs(14)
                    dve.wait_ge(eexp_done, i * 2 + half + 1)
                    step(nc.vector.tensor_tensor(topp[:, T, :], eprob[:, T, :], top[:, T, :], ALU.mult))
                    step(nc.vector.tensor_reduce(esum[:, T], eprob[:, T, :], AX.X, ALU.add))
                    needs(16)
                    step(nc.vector.tensor_reduce(tsum[:, T], topp[:, T, :], AX.X, ALU.add))
                    needs(17)
                    step(nc.vector.scalar_tensor_tensor(tden[:, T], esum[:, T], 1e-8, tsum[:, T], ALU.mult, ALU.add))
                    needs(18)
                    step(nc.vector.reciprocal(trec[:, T], tden[:, T]))
                    needs(19)
                    step(nc.vector.tensor_tensor(wsel[:, T, :], topp[:, T, :], trec[:, T].unsqueeze(2).to_broadcast(
                        [P, HT, EG]), ALU.mult))

            def forward(i, st):
                kind = st[0]
                if kind == "in":
                    q = st[1]
                    ex, c, half = IN_STEPS[q]
                    ab = pair[q % 2]
                    if later(i) or q:
                        dve.wait_ge(hid_made, i * NIN + q)
                    if later(i) or q >= 4:
                        dve.wait_ge(ex_step, (i * TILES + HT * (q // 4)) * EG)
                    dve.wait_ge(tanh_done, i * NIN + q + 1)
                    nc.vector.scalar_tensor_tensor(from_dve[:, q % 2, :], from_act[:, q % 2, :], 1.0, ab[:, 0:HALF],
                                                   ALU.add, ALU.mult).then_inc(gate_made, 1)
                    dve.wait_ge(gate_made, i * NIN + q + 1)
                    if ex and (later(i) or half):
                        dve.wait_ge(hidl_made, i * 4 + 2 * half)
                    elif later(i) or half:
                        dve.wait_ge(shared_ready, i * 2 + half)
                    nc.vector.scalar_tensor_tensor(hid[:, ex, c, :], from_dve[:, q % 2, :], 0.5,
                                                   ab[:, HALF:2 * HALF], ALU.mult, ALU.mult).then_inc(hid_made, 1)
                elif kind == "shared":
                    half = st[1]
                    dve.wait_ge(shared_ready, i * 2 + half + 1)
                    nc.vector.tensor_tensor(acc[:, tiles(half), :], (b7, b6)[half][:].rearrange("p (t c) -> p t c", c=P),
                                            h2[:, tiles(half), :], ALU.add).then_inc(base_made, 1)
                elif kind == "expert":
                    t = st[1]
                    slot = t % 2
                    if t % HT == 0:
                        dve.wait_ge(hid_made, i * NIN + (t // HT + 1) * 4)
                        dve.wait_ge(base_made, i * 2 + t // HT + 1)
                        dve.wait_ge(route_step, (i * 2 + t // HT + 1) * ROUTE)
                    dve.wait_ge(sela_made, i * TILES + t + 1)
                    nc.vector.scalar_tensor_tensor(from_dve[:, slot, :], pair[slot][:, HALF:2 * HALF], gm[:, t, 1:2],
                                                   from_act[:, slot, :], ALU.mult, ALU.add).then_inc(sel_made, 1)
                    dve.wait_ge(sel_made, i * TILES + t + 1)
                    for e in range(EG):
                        if e:
                            dve.wait_ge(ex_step, (i * TILES + t) * EG + e)
                        nc.vector.scalar_tensor_tensor(acc[:, t, :], from_dve[:, slot, e * P:(e + 1) * P],
                                                       wsel[:, t, e:e + 1], acc[:, t, :],
                                                       ALU.mult, ALU.add).then_inc(ex_step, 1)

            def stage(i, st):
                if st[0] == "score":
                    score(i, st[1])
                elif st[0] == "turn":
                    maxima_split(i, st[1])
                elif of_next_image(st):
                    front(i, st[0], st[1])
                elif st[0] in ("in", "counts", "shared", "expert"):
                    forward(i, st)
                else:
                    post(i, st)

            def image(i):
                for st in PERIOD:
                    stage(i + of_next_image(st), st)

            dve.wait_ge(const_made, CONSTS)
            for st in FIRST:
                stage(0, st)
            dve.wait_ge(w_in2, 9 * 16)
            image(0)
            with dve.Fori(1, B - 1) as i:
                image(i)
            for st in LAST:
                stage(B - 1, st)

        @block.scalar
        def _(act):
            def front(i, kind, half):
                if kind == "turn1":
                    if later(i):
                        act.wait_ge(z2l_made, i * 2 - 1 + half)
                    act.wait_ge(front_mm, front_step(i, "turn1", half))
                    src = (b7, b6)[half]
                    nc.scalar.copy(zt[:, halfs(half)], src[:]).then_inc(zt_made, 1)
                    nc.scalar.copy(zt_h[:, halfs(half)], src[:]).then_inc(zth_made, 1)
                if kind in ("q", "k"):
                    w = "qk".index(kind)
                    src, bias = (b6 if half and w else b7), (bq_sb, bk_sb)[w]
                    act.wait_ge(front_mm, front_step(i, kind, half))
                    nc.scalar.activation(qk[:, w, halfs(half)], src[:], ACT.Identity,
                                         bias=bias[:, 0:1]).then_inc(qk_made, 1)
                    nc.scalar.activation(qk_h[:, w, halfs(half)], src[:], ACT.Identity,
                                         bias=bias[:, 0:1]).then_inc(qkh_made, 1)

            def take(i, u):
                g, half = UNITS[u]
                act.wait_ge(pv_done, i * NP_ + UNIT_LAST[u] + 1)
                nc.scalar.copy(ot[:, g, halfs(half)], b6[:]).then_inc(pv_taken, 1)

            def prob(i, k, part):
                u, kt = PROB_STEPS[k]
                q0, _ = prob_columns(k)
                if part == 0 and (k >= PT_SLOTS or later(i)):
                    act.wait_ge(pv_done, i * NP_ + max(0, k - PT_SLOTS + 1))
                for j in (2 * part, 2 * part + 1):
                    p = k * G4 + j
                    act.wait_ge(st_ready, i * NP_ * G4 + p + 1)
                    nc.scalar.activation(pt[:, k % PT_SLOTS, j, q0:HALF], (b4, b5)[p % 2][:, q0:HALF], ACT.Exp,
                                         scale=0.25).then_inc(exp_done, 1)

            def post(i, st):
                kind, half = st[0], st[1]
                if kind == "ant":
                    act.wait_ge(ant_ready, i * 2 + half + 1)
                    nc.scalar.copy(ant[:, halfs(half)], b6[:] if half else pair[1][:, 0:HALF]).then_inc(ant_made, 1)
                if kind == "z2t":
                    src = b6[:] if half else pair[0][:, 0:HALF]
                    act.wait_ge(z2t_ready, i * 2 + half + 1)
                    for dst, made in ((z2t, z2t_made), (z2t_h, z2h_made)):
                        nc.scalar.activation(dst[:, halfs(half)], src, ACT.Identity, bias=lnb_sb[:, 0:1],
                                             scale=lns_sb[:, 0:1]).then_inc(made, 1)
                if kind == "route" and st[2] == 0:
                    act.wait_ge(route_step, (i * 2 + half) * ROUTE + 9)
                    nc.scalar.activation(eprob[:, tiles(half), :], esub[:, tiles(half), :], ACT.Exp).then_inc(eexp_done, 1)

            def forward(i, st):
                kind = st[0]
                if kind == "in":
                    q = st[1]
                    act.wait_ge(in_ready, i * NIN + q + 1)
                    nc.scalar.activation(from_act[:, q % 2, :], pair[q % 2][:, 0:HALF], ACT.Tanh,
                                         scale=0.5).then_inc(tanh_done, 1)
                    if IN_STEPS[q - 1][0] == 1 and q % 4:
                        _, c, half = IN_STEPS[q - 1]
                        act.wait_ge(hid_made, i * NIN + q)
                        if later(i) or half:
                            act.wait_ge(ex_ready, i * TILES + half * HT)
                        nc.scalar.copy(hid_h[:, c, :], hid[:, 1, c, :]).then_inc(hidh_made, 1)
                elif kind == "expert":
                    t = st[1]
                    slot = t % 2
                    act.wait_ge(ex_ready, i * TILES + t + 1)
                    if t % HT == 0:
                        act.wait_ge(route_step, (i * 2 + t // HT + 1) * ROUTE)
                    nc.scalar.mul(from_act[:, slot, :], pair[slot][:, 0:HALF], gm[:, t, 0:1]).then_inc(sela_made, 1)
                elif kind == "counts":
                    half = st[1]
                    act.wait_ge(cnt_ready, i * 2 + half + 1)
                    if later(i) or half:
                        act.wait_ge(base_made, i * 2 + half)
                    nc.scalar.copy(cnt_t[:], b7[0:EXPERTS + 1, :]).then_inc(cnt_taken, 1)

            def stage(i, st):
                if st[0] == "prob":
                    prob(i, st[1], st[2])
                elif st[0] == "take":
                    take(i, st[1])
                elif st[0] in ("turn1", "q", "k"):
                    front(i, st[0], st[1])
                elif st[0] in ("in", "counts", "expert"):
                    forward(i, st)
                elif st[0] in ("ant", "z2t", "route"):
                    post(i, st)

            def image(i):
                for st in PERIOD:
                    stage(i + of_next_image(st), st)

            act.wait_ge(w_in1, 9 * 16)
            for st in FIRST:
                stage(0, st)
            act.wait_ge(w_in2, 9 * 16)
            nc.scalar.copy(win_h[:], win_sb).then_inc(wsplit_h, 1)
            nc.scalar.copy(wex_h[:], wex_sb).then_inc(wsplit_h, 1)
            image(0)
            with act.Fori(1, B - 1) as i:
                image(i)
            for st in LAST:
                stage(B - 1, st)

        @block.gpsimd
        def _(pool):
            zeroed = sem_zero
            nc.gpsimd.memset(ident[:], 0.0).then_inc(zeroed, 1)
            nc.gpsimd.memset(causal[:], 0.0).then_inc(zeroed, 1)
            nc.gpsimd.memset(tri[:], 1.0).then_inc(zeroed, 1)
            nc.gpsimd.memset(v[:], 0.0).then_inc(zeroed, 1)
            nc.gpsimd.memset(words(q_stack[:]), 0.0).then_inc(zeroed, 1)
            nc.gpsimd.memset(words(k_stack[:]), 0.0).then_inc(zeroed, 1)
            pool.wait_ge(zeroed, 6)
            nc.gpsimd.affine_select(out=ident[:], in_=ident[:], compare_op=ALU.not_equal, fill=1.0, base=0,
                                    pattern=[[-1, P]], channel_multiplier=1).then_inc(const_made, 1)
            nc.gpsimd.affine_select(out=causal[:, S - P:S], in_=causal[:, S - P:S], compare_op=ALU.is_ge, fill=MASK,
                                    base=0, pattern=[[-1, P]], channel_multiplier=1).then_inc(const_made, 1)
            nc.gpsimd.affine_select(out=tri[:].rearrange("p (i j) -> p i j", j=EG),
                                    in_=tri[:].rearrange("p (i j) -> p i j", j=EG), compare_op=ALU.is_gt, fill=0.0,
                                    base=0, pattern=[[1, EG], [-1, EG]], channel_multiplier=0).then_inc(const_made, 1)
            nc.gpsimd.memset(v[:, :, :, DH:DH + 1], 1.0).then_inc(const_made, 1)
            nc.gpsimd.memset(half_pow[:], -0.5).then_inc(const_made, 1)
            nc.gpsimd.memset(words(minus1), -1.0).then_inc(const_made, 1)
            nc.gpsimd.memset(cnt[:, :, EXPERTS:EXPERTS + 1], 1.0).then_inc(const_made, 1)
            pool.wait_ge(const_made, CONSTS)
            pool.wait_ge(w_in1, 9 * 16)

            def front(i, kind, half):
                if kind == "emb":
                    alone(pool, mv_made, i * TILES + (half + 1) * HT)
                    nc.gpsimd.tensor_scalar(var1[:, tiles(half)], mv[:, tiles(half), 1], EPS, None,
                                            ALU.add).then_inc(var_made, 1)
                    pool.wait_ge(var_made, i * 2 + half + 1)
                    nc.gpsimd.tensor_tensor(rs1[:, tiles(half)], var1[:, tiles(half)], half_pow[:, tiles(half)],
                                            ALU.pow).then_inc(rs_made, 1)
                if kind == "turn1":
                    pool.wait_ge(zth_made, i * 2 + half + 1)
                    nc.gpsimd.tensor_tensor(zt_l[:, halfs(half)], zt[:, halfs(half)], zt_h[:, halfs(half)].bitcast(F32),
                                            ALU.subtract).then_inc(ztl_made, 1)
                if kind in ("q", "k"):
                    w = "qk".index(kind)
                    pool.wait_ge(qkh_made, i * 4 + 2 * half + w + 1)
                    nc.gpsimd.tensor_tensor(qk_l[:, w, halfs(half)], qk[:, w, halfs(half)],
                                            qk_h[:, w, halfs(half)].bitcast(F32), ALU.subtract).then_inc(qkl_made, 1)

            def mask(i, k):
                q0, _ = prob_columns(k)
                alone(pool, exp_done, i * NP_ * G4 + (k + 1) * G4)
                d = pt[:, k % PT_SLOTS, :, q0:q0 + P]
                nc.gpsimd.affine_select(out=d, in_=d, compare_op=ALU.is_ge, fill=0.0, base=0,
                                        pattern=[[0, G4], [1, P]], channel_multiplier=-1).then_inc(mask_done, 1)

            def post(i, st):
                kind, half = st[0], st[1]
                T = tiles(half)
                if kind == "oproj":
                    base = (i * 2 + half) * LN_STEPS
                    var = mv2[:, T, 1]
                    alone(pool, mv2_made, i * TILES + (half + 1) * HT)
                    nc.gpsimd.tensor_scalar(t1[:, T], var, EPS, None, ALU.add).then_inc(ln2_step, 1)
                    pool.wait_ge(ln2_step, base + 1)
                    nc.gpsimd.tensor_tensor(t2[:, T], t1[:, T], half_pow[:, T], ALU.pow).then_inc(ln2_step, 1)
                    pool.wait_ge(ln2_step, base + 2)
                    nc.gpsimd.tensor_tensor(t3[:, T], var, t2[:, T], ALU.mult).then_inc(ln2_step, 1)
                    pool.wait_ge(ln2_step, base + 3)
                    nc.gpsimd.tensor_tensor(t4[:, T], t3[:, T], t2[:, T], ALU.mult).then_inc(ln2_step, 1)
                    alone(pool, ln2_step, base + 4)
                    nc.gpsimd.tensor_scalar(t4e[:, T], t4[:, T], EPS, None, ALU.add).then_inc(ln2_step, 1)
                    pool.wait_ge(ln2_step, base + 5)
                    nc.gpsimd.tensor_tensor(t5[:, T], t4e[:, T], half_pow[:, T], ALU.pow).then_inc(ln2_step, 1)
                    pool.wait_ge(ln2_step, base + 6)
                    nc.gpsimd.tensor_tensor(t6[:, T], t5[:, T], t2[:, T], ALU.mult).then_inc(ln2_step, 1)
                if kind == "z2t":
                    pool.wait_ge(z2h_made, i * 2 + half + 1)
                    nc.gpsimd.tensor_tensor(z2t_l[:, halfs(half)], z2t[:, halfs(half)],
                                            words(z2t_h[:, halfs(half)]), ALU.subtract).then_inc(z2l_made, 1)

            def split_hidden(i, q):
                ex, c, half = IN_STEPS[q - 1]
                if ex and q % 4:
                    pool.wait_ge(hidh_made, i * 4 + 2 * half + c + 1)
                    nc.gpsimd.tensor_tensor(hid_l[:, c, :], hid[:, 1, c, :], words(hid_h[:, c, :]),
                                            ALU.subtract).then_inc(hidl_made, 1)

            def stage(i, st):
                if st[0] == "prob":
                    if st[1] in DIAG and st[2] == 1:
                        mask(i, st[1])
                elif st[0] in ("emb", "turn1", "q", "k"):
                    front(i, st[0], st[1])
                elif st[0] == "in":
                    split_hidden(i, st[1])
                elif st[0] in ("oproj", "z2t"):
                    post(i, st)

            def image(i):
                for st in PERIOD:
                    stage(i + of_next_image(st), st)

            for st in FIRST:
                stage(0, st)
            pool.wait_ge(wsplit_h, 1)
            nc.gpsimd.tensor_tensor(win_l[:], win_sb, win_h[:].bitcast(F32), ALU.subtract).then_inc(wsplit_l, 1)
            pool.wait_ge(wsplit_h, 2)
            nc.gpsimd.tensor_tensor(wex_l[:], wex_sb, wex_h[:].bitcast(F32), ALU.subtract).then_inc(wsplit_l, 1)
            image(0)
            with pool.Fori(1, B - 1) as i:
                image(i)
            for st in LAST:
                stage(B - 1, st)


def position_table():
    import math
    position = np.arange(2 * S, dtype=np.float32)[:, None]
    div_term = np.exp(np.arange(0, P, 2, dtype=np.float32) * (-math.log(10000.0) / P))
    pe = np.zeros((2 * S, P), dtype=np.float32)
    pe[:, 0::2] = np.sin(position * div_term)
    pe[:, 1::2] = np.cos(position * div_term)
    return np.ascontiguousarray(pe[:S].reshape(TILES, P, P).transpose(1, 0, 2))


def kernel(**inputs):
    import numpy as _np
    import concourse.bacc as _bacc
    from concourse import mybir as _mybir
    from concourse.bass_utils import run_bass_kernel_spmd as _run

    a = {k: _np.asarray(w) for k, w in inputs.items()}

    def rows(w):
        return _np.broadcast_to(w[None, :], (P, w.shape[0]))

    def column(w):
        return w.reshape(P, 1)

    def by_pairs(w):
        w = w.reshape(-1, HEADS // 2, 2, DH)
        return w.transpose(0, 2, 3, 1).reshape(-1, P)

    laid = {
        "x_t": a["x"].reshape(B * S, F).T,
        "tok_w": a["L0_tok_W"],
        "pos": position_table(),
        "wq": by_pairs(a["L0_attn_Wq"]), "wk": by_pairs(a["L0_attn_Wk"]), "wv": a["L0_attn_Wv"], "wo": a["L0_attn_Wo"],
        "bq": column(by_pairs(a["L0_attn_bq"])), "bk": column(by_pairs(a["L0_attn_bk"])),
        "bv": rows(a["L0_attn_bv"]), "bo": rows(a["L0_attn_bo"]),
        "ln_s": column(a["L0_ffn_ln_scale"]), "ln_b": column(a["L0_ffn_ln_bias"]),
        "w_in": _np.concatenate([a["L0_ffn_shared_in_w"], a["L0_ffn_expert_in_w"]], 0).T,
        "w_shared": a["L0_ffn_shared_out_w"].T.reshape(HID // P, P, P).transpose(1, 0, 2),
        "w_expert": a["L0_ffn_expert_out_weight"].transpose(2, 0, 1).reshape(HID // P, P, EXPERTS * P).transpose(1, 0, 2),
        "w_bias": _np.concatenate([a["L0_ffn_expert_out_bias"], a["L0_ffn_shared_out_b"][None, :]], 0),
        "w_gate": _np.concatenate([a["L0_ffn_group_gate_w"], a["L0_ffn_expert_gate_w"]], 0).T,
        "b_gate": rows(_np.concatenate([a["L0_ffn_group_bias"], a["L0_ffn_expert_bias"]])),
    }
    nc = _bacc.Bacc("TRN2", target_bir_lowering=False, num_devices=1)
    arrays, args = {}, []
    for name, w in laid.items():
        w = _np.ascontiguousarray(w)
        arrays[name] = w
        args.append(nc.dram_tensor(name, w.shape, _mybir.dt.from_np(w.dtype), kind="ExternalInput").ap())
    args.append(nc.dram_tensor("out", (B, S, P), _mybir.dt.float32, kind="ExternalOutput").ap())
    build(nc, *args)
    r = _run(nc, [arrays], core_ids=[0])
    return r.results[0]["out"]
```

```python
from contextlib import ExitStack

import numpy as np
import concourse.bass as bass
from concourse import mybir

F32 = mybir.dt.float32
F32R = mybir.dt.float32r
ALU = mybir.AluOpType
ACT = mybir.ActivationFunctionType
AX = mybir.AxisListType

P = 128
B, S, F = 8, 1024, 29
TILES = S // P
HALF = 512
HT = HALF // P
HEADS, DH = 8, 16
G4 = 4
HID = 256
EXPERTS, GROUPS, EG = 8, 2, 4
NGATE = GROUPS + EXPERTS
GATE_W = 32
ODD = 64
STACK = ODD + 3 * DH
SHIFT = P - 2
EPS = 1e-5
MASK = -100000.0
VW = 32

UNITS = [(0, 0), (1, 0), (0, 1), (1, 1)]
SCORE_STEPS = [(u, HT * half + t, j) for u, (g, half) in enumerate(UNITS) for t in range(HT) for j in range(G4)]
PROB_STEPS = [(u, kt) for u, (g, half) in enumerate(UNITS) for kt in range(HT * (half + 1))]
NS, NP_, NU = len(SCORE_STEPS), len(PROB_STEPS), len(UNITS)
UNIT_S = NS // NU
DIAG = [k for k, (u, kt) in enumerate(PROB_STEPS) if kt >= HT * UNITS[u][1]]
UNIT_LAST = [max(k for k, (u, _) in enumerate(PROB_STEPS) if u == v) for v in range(NU)]
KEYS_USED = max(k for k, (_, kt) in enumerate(PROB_STEPS) if kt < HT)
PT_SLOTS = 2


def prob_columns(k):
    u, kt = PROB_STEPS[k]
    q0 = max(0, kt * P - UNITS[u][1] * HALF)
    return q0, min(q0, HALF - 256)


def later(i):
    return not (isinstance(i, int) and i == 0)


IN_STEPS = [(kind, c, half) for half in range(2) for kind in (1, 0) for c in range(HID // P)]
NIN = len(IN_STEPS)
FRONT_STEPS = [("emb", 0), ("turn1", 0), ("q", 0), ("k", 0), ("v", 0), ("emb", 1), ("turn1", 1), ("q", 1), ("k", 1),
               ("v", 1)]
NF = len(FRONT_STEPS)
LN_STEPS = 2
COMBINE = 3
ROUTE = 20


def of_next_image(st):
    return (st[0] in ("emb", "turn1", "q", "k", "v") or st[0] == "score" and st[1] < 2 * UNIT_S or
            st[0] == "turn" and st[1] < 2)


def streams():
    pass1 = []
    for u in (2, 3, 0, 1):
        pass1 += [("score", s) for s in range(u * UNIT_S, (u + 1) * UNIT_S)] + [("turn", u)]
    pass2 = [("prob", k, j) for k in range(NP_) for j in range(G4)]
    weighing = []
    for k in range(NP_):
        weighing.append(("weigh", k))
        if k in UNIT_LAST:
            weighing.append(("take", UNIT_LAST.index(k)))
    middle, forward = [], []
    for half in range(2):
        middle += [("to", half), ("ant", half), ("oproj", half), ("emb", half), ("z2t", half), ("gates", half),
                   ("route", half, 0), ("turn1", half), ("route", half, 1), ("route", half, 2), ("q", half), ("k", half)]
        middle += [("v", 1), ("counts", 1), ("shared", 1)] if half else [("counts", 0), ("shared", 0), ("v", 0)]
        forward += [("in", q, ab) for q in range(4 * half, 4 * half + 4) for ab in range(2)]
        forward += [("expert", t, g) for t in range(HT * half, HT * half + HT) for g in range(GROUPS)]
    combine = [("combine", t) for t in range(TILES)]
    return {"s": pass1, "p": pass2, "w": weighing, "m": middle, "f": forward, "c": combine}


WEAVE = (
    "ssppspspspsppswspsppsppwsppsppwsppspwpwsppsppwsspspwppsppspspwpspwpspsppwspspwpssppwppssppwppsps"
    "ppwppmpspwppmwppmppwppmppppwwppmwppmppmwppfpmfppfwpmpmmfpwpmfppfffppmwppfppmpwppppmwsswsswssmssf"
    "mcssfssmfcmfffmssfcmcmfmmssffsfmmfsfsmmfsffssfssfmssfssmccssfsfsfsfscc"
)


def period(weave, woven):
    left = {name: iter(stream) for name, stream in woven.items()}
    return [next(left[name]) for name in weave]


PERIOD = period(WEAVE, streams())
FIRST = sorted((st for st in PERIOD if of_next_image(st)),
               key=lambda st: (3 if st[0] == "turn" or st[0] == "score" and st[1] >= 6 else
                               2 if st in (("q", 1), ("k", 1), ("v", 1)) else 1 if st[0] == "score" else 0))
LAST_WEAVE = (
    "sppssppssppswspsppsppspwsppsppwsppwsppswppsppwsspspwppspsppspwpspspwpswppssppwpssppwppssppwppsps"
    "ppwppsmppwppmppwppppwppmppwwpppwpppmpwpmppmwppffmppwppfpfpfpwmpfppfpfpmwppwppmwwfmfmcfmfffccfmfm"
    "cfmfffffmffmfffmfmccffffcc"
)
LAST = period(LAST_WEAVE, {name: [st for st in stream if not of_next_image(st)] for name, stream in streams().items()})


def build(nc, x_t, tok_w, pos, wq, wk, wv, wo, bq, bk, bv, bo, ln_s, ln_b, w_in, w_shared, w_expert, w_bias,
          w_gate, b_gate, out):
    with ExitStack() as ctx:
        def sb(name, shape, dt=F32):
            return ctx.enter_context(nc.sbuf_tensor(name, shape, dt))

        def sem(name):
            return ctx.enter_context(nc.semaphore(name))

        bank = [ctx.enter_context(nc.psum_tensor(f"bank{n}", [P, HALF], F32)) for n in (4, 5, 6, 7)]
        pair = [ctx.enter_context(nc.psum_tensor(f"pair{n}", [P, 2 * HALF], F32)) for n in range(2)]
        b4, b5, b6, b7 = bank

        ident = sb("ident", [P, P])
        causal = sb("causal", [P, S])
        tri = sb("tri", [P, EG * EG])
        half_pow = sb("half_pow", [P, TILES])
        pos_sb = sb("pos_sb", [P, TILES, P])
        tokw_sb = sb("tokw_sb", [F, P])
        wq_sb, wk_sb, wv_sb, wo_sb = (sb(n, [P, P]) for n in ("wq_sb", "wk_sb", "wv_sb", "wo_sb"))
        wqk_h = sb("wqk_h", [P, 2, P], F32R)
        wqk_l = sb("wqk_l", [P, 2, P], F32R)
        bq_sb, bk_sb, lns_sb, lnb_sb = (sb(n, [P, 1]) for n in ("bq_sb", "bk_sb", "lns_sb", "lnb_sb"))
        bv_sb, bo_sb = sb("bv_sb", [P, P]), sb("bo_sb", [P, P])
        bgate_sb = sb("bgate_sb", [P, NGATE])
        wgate_sb = sb("wgate_sb", [P, GATE_W])
        wbias_sb = sb("wbias_sb", [EXPERTS + 1, P])
        wshared_sb = sb("wshared_sb", [P, HID // P, P])
        win_h, win_l = sb("win_h", [P, 4 * HID], F32R), sb("win_l", [P, 4 * HID], F32R)
        wex_h = sb("wex_h", [P, HID // P, EXPERTS * P], F32R)
        wex_l = sb("wex_l", [P, HID // P, EXPERTS * P], F32R)

        x_sb = sb("x_sb", [F, S])
        h = sb("h", [P, TILES, P])
        stats = sb("stats", [P, TILES, 6])
        mv = sb("mv", [P, TILES, 2])
        var1 = sb("var1", [P, TILES])
        rs1 = sb("rs1", [P, TILES])
        z = sb("z", [P, TILES, P])
        zt = sb("zt", [P, S])
        zt_h, zt_l = sb("zt_h", [P, S], F32R), sb("zt_l", [P, S], F32R)
        qk_h, qk_l = sb("qk_h", [P, 2, S], F32R), sb("qk_l", [P, 2, S], F32R)
        v = sb("v", [P, TILES, HEADS, VW])
        q_stack = sb("q_stack", [P, 2, HEADS, HALF], F32R)
        k_stack = sb("k_stack", [P, HEADS // 2, S], F32R)
        mx = sb("mx", [P, NS])
        mrow_h, mrow_l = sb("mrow_h", [UNIT_S, NU, P], F32R), sb("mrow_l", [UNIT_S, NU, P], F32R)
        pt = sb("pt", [P, PT_SLOTS, G4, HALF])
        wex_sb = pt[:, 0, :, :].rearrange("p (c x) q -> p c (x q)", c=HID // P)
        win_sb = pt[:, 1, 0:2, :].rearrange("p x q -> p (x q)")
        ot = sb("ot", [P, 2, S])
        qk = ot
        rec = sb("rec", [P, TILES, HEADS])
        an, ant = z, zt
        h2 = sb("h2", [P, TILES, P])
        stats2 = sb("stats2", [P, TILES, 6])
        mv2 = sb("mv2", [P, TILES, 2])
        var2, rs2 = sb("var2", [P, TILES]), sb("rs2", [P, TILES])
        z2, z2t = z, zt
        z2t_h, z2t_l = sb("z2t_h", [P, S], F32R), sb("z2t_l", [P, S], F32R)
        gl = sb("gl", [P, TILES, NGATE])
        gm = sb("gm", [P, TILES, GROUPS])
        both = sb("both", [P, TILES, GROUPS, EG])
        esel = sb("esel", [P, TILES, EG])
        emax = sb("emax", [P, TILES])
        esub = sb("esub", [P, TILES, EG])
        eprob = sb("eprob", [P, TILES, EG])
        esum = sb("esum", [P, TILES])
        cmp_gt, cmp_eq = sb("cmp_gt", [P, TILES, EG * EG]), sb("cmp_eq", [P, TILES, EG * EG])
        cmp_tie, cmp_all = sb("cmp_tie", [P, TILES, EG * EG]), sb("cmp_all", [P, TILES, EG * EG])
        rank = sb("rank", [P, TILES, EG])
        top = sb("top", [P, TILES, EG])
        topp = sb("topp", [P, TILES, EG])
        tsum, tden, trec = sb("tsum", [P, TILES]), sb("tden", [P, TILES]), sb("trec", [P, TILES])
        wsel = sb("wsel", [P, TILES, EG])
        cnt = sb("cnt", [P, TILES, EXPERTS + 1])
        cnt_t = sb("cnt_t", [EXPERTS + 1, HALF])
        from_act = sb("from_act", [P, 2, HALF])
        from_dve = sb("from_dve", [P, 2, HALF])
        hid = sb("hid", [P, 2, HID // P, HALF])
        hid_h = sb("hid_h", [P, HID // P, HALF], F32R)
        hid_l = sb("hid_l", [P, HID // P, HALF], F32R)
        minus1 = hid_l[0:2, :, :]
        acc = h2

        w_in0 = sem("w_tokens_loaded")
        w_in1 = sem("w_front_loaded")
        w_in2 = sem("w_rest_loaded")
        const_made = sem("const_made")
        ones_in = sem("minus_ones_in_stack")
        wsplit_qk = sem("wsplit_qk")
        wsplit_h = sem("wsplit_h")
        wsplit_l = sem("wsplit_l")
        x_in = sem("x_in")
        front_mm = sem("front_mm")
        h_made = sem("h_made")
        zt_made, qk_made = sem("zt_made"), sem("qk_made")
        hb_made = sem("hb_made")
        stat1 = sem("stat1")
        mv_made = sem("mv_made")
        var_made = sem("var_made")
        rs_made = sem("rs_made")
        z_made = sem("z_made")
        zth_made, ztl_made = sem("zth_made"), sem("ztl_made")
        qkh_made, qkl_made = sem("qkh_made"), sem("qkl_made")
        v_made = sem("v_made")
        stack_in = [sem(f"stack_in_{half}") for half in range(2)]
        s_ready, s_taken = sem("scores_ready"), sem("scores_taken")
        m_turned, mh_made, ml_made = sem("max_turned"), sem("mh_made"), sem("ml_made")
        m_in = [sem(f"max_in_stack_{u}") for u in range(NU)]
        st_ready, exp_done, mask_done = sem("st_ready"), sem("exp_done"), sem("mask_done")
        pv_done, pv_taken = sem("pv_done"), sem("pv_taken")
        to_ready, rec_made, an_made = sem("to_ready"), sem("rec_made"), sem("an_made")
        ant_ready, ant_made = sem("ant_ready"), sem("ant_made")
        o_ready, h2_made = sem("o_ready"), sem("h2_made")
        stat2, mv2_made, ln2_step, z2_made = sem("stat2"), sem("mv2_made"), sem("ln2_step"), sem("z2_made")
        z2t_ready, z2t_made = sem("z2t_ready"), sem("z2t_made")
        z2h_made, z2l_made = sem("z2h_made"), sem("z2l_made")
        gl_ready, route_step, eexp_done = sem("gl_ready"), sem("route_step"), sem("eexp_done")
        in_ready, tanh_done, gate_made, hid_made = sem("in_ready"), sem("tanh_done"), sem("gate_made"), sem("hid_made")
        hidh_made, hidl_made = sem("hidh_made"), sem("hidl_made")
        cnt_ready, cnt_taken = sem("cnt_ready"), sem("cnt_taken")
        shared_ready, base_made = sem("shared_ready"), sem("base_made")
        ex_ready, sela_made, sel_made, weighted, ex_step = (
            sem(n) for n in ("ex_ready", "sela_made", "sel_made", "weighted", "ex_step"))
        out_done = [sem(f"out_done_{half}") for half in range(2)]
        zeroed, ident_made = sem("zeroed"), sem("ident_made")
        stacks_zeroed = sem("stacks_zeroed")
        went_on = sem("went_on")

        out_v = out.rearrange("b (t p) c -> b p t c", p=P)
        CONSTS = 6

        def halfs(half):
            return slice(half * HALF, (half + 1) * HALF)

        def tiles(half):
            return slice(half * HT, (half + 1) * HT)

        def front_step(i, what, half):
            return i * NF + FRONT_STEPS.index((what, half)) + 1

        def slot_summed(i, q):
            return (i * TILES + q // 4 * HT - 1 + q % 4) * COMBINE

        def words(ap):
            return ap.bitcast(F32)

        def alone(eng, semaphore, value):
            eng.wait_ge(semaphore, value)
            eng.sem_inc(went_on, 1)

        block = ctx.enter_context(nc.Block())

        @block.sync
        def _(sp):
            def load_x(i):
                sp.dma_start(x_sb[:], x_t[:, bass.ds(i * S, S)]).then_inc(x_in, 16)

            load_x(0)
            for dst, src in ((tokw_sb, tok_w), (pos_sb, pos)):
                sp.dma_start(dst[:], src).then_inc(w_in0, 16)
            for dst, src in ((wq_sb, wq), (wk_sb, wk), (bq_sb, bq), (bk_sb, bk),
                             (wv_sb, wv), (bv_sb, bv), (bo_sb, bo)):
                sp.dma_start(dst[:], src).then_inc(w_in1, 16)
            for dst, src in ((wo_sb, wo), (lns_sb, ln_s), (lnb_sb, ln_b), (win_sb, w_in), (wshared_sb, w_shared),
                             (wex_sb, w_expert), (wbias_sb, w_bias), (wgate_sb, w_gate), (bgate_sb, b_gate)):
                sp.dma_start(dst if dst is win_sb or dst is wex_sb else dst[:], src).then_inc(w_in2, 16)
            sp.wait_ge(const_made, CONSTS)
            sp.wait_ge(stacks_zeroed, 3)
            for n in range(HEADS // 2):
                sp.dma_start(words(k_stack[SHIFT:P, n, :]), words(minus1.rearrange("r c n -> r (c n)"))).then_inc(ones_in, 16)

            def stacks(i, half, w):
                if w == 0:
                    sp.wait_ge(qkh_made, i * 4 + 2 * half + 2)
                    sp.wait_ge(qkl_made, i * 4 + 2 * half + 2)
                for n, part in enumerate((qk_h, (qk_h, qk_l)[w], (qk_l, qk_h)[w])):
                    for odd in range(2):
                        to = slice(odd * ODD + n * DH, odd * ODD + (n + 1) * DH)
                        stack = k_stack[to, :, halfs(half)] if w else q_stack[to, half, odd::2, :]
                        rows = part[odd * (P // 2):(odd + 1) * (P // 2), w, halfs(half)]
                        sp.dma_start(words(stack), words(rows)).then_inc(stack_in[half], 16)

            def maxima(i, u):
                g, half = UNITS[u]
                sp.wait_ge(ml_made, i * NU + u + 1)
                for row, part in ((SHIFT, mrow_h), (SHIFT + 1, mrow_l)):
                    dst = q_stack[row:row + 1, half, g * G4:(g + 1) * G4, :]
                    sp.dma_start(words(dst), words(part[:, u, :])).then_inc(m_in[u], 16)

            def store(i, half):
                sp.wait_ge(ex_step, (i * TILES + (half + 1) * HT) * COMBINE)
                sp.dma_start(out_v[i, :, tiles(half), :], acc[:, tiles(half), :]).then_inc(out_done[half], 16)

            def stage(i, st, loads=True):
                if st[0] == "turn":
                    maxima(i, st[1])
                elif st == ("k", 0):
                    stacks(i, 0, 0)
                    if not later(i):
                        stacks(i, 0, 1)
                elif st == ("k", 1):
                    stacks(i, 1, 0)
                    stacks(i, 1, 1)
                    if loads:
                        load_x(i + 1)
                elif st == ("combine", 3):
                    store(i, 0)
                elif st == ("combine", 7):
                    store(i, 1)

            def keys(i):
                sp.wait_ge(exp_done, i * NP_ * G4 + (KEYS_USED + 1) * G4)
                stacks(i + 1, 0, 1)

            def image(i, loads):
                for n, st in enumerate(PERIOD):
                    stage(i + of_next_image(st), st, loads)
                    if n == max(PERIOD.index(("k", 0)), PERIOD.index(("prob", KEYS_USED, G4 - 1))):
                        keys(i)

            for st in FIRST:
                stage(0, st)
            image(0, True)
            with sp.Fori(1, B - 2) as i:
                image(i, True)
            image(B - 2, False)
            for st in LAST:
                stage(B - 1, st)
            for half in range(2):
                sp.wait_ge(out_done[half], B * 16)

        @block.tensor
        def _(pe):
            def split_mm(dst, wh, wl, xh, xl, first=True, last=True):
                nc.tensor.matmul(dst, wh, xh, start=first, stop=False)
                nc.tensor.matmul(dst, wl, xh, start=False, stop=False)
                return nc.tensor.matmul(dst, wh, xl, start=False, stop=last)

            def front(i, kind, half):
                if kind == "emb":
                    pe.wait_ge(x_in, (i + 1) * 16)
                    if later(i) and half == 0:
                        pe.wait_ge(ml_made, i * NU)
                    if later(i) and half == 1:
                        pe.wait_ge(ant_made, i * 2)
                    for t in range(HT):
                        mm = nc.tensor.matmul((b7, b6)[half][:, t * P:(t + 1) * P],
                                              x_sb[:, (half * HT + t) * P:(half * HT + t + 1) * P],
                                              tokw_sb[:], start=True, stop=True)
                    mm.then_inc(front_mm, 1)
                if kind == "turn1":
                    pe.wait_ge(z_made, i * TILES + (half + 1) * HT)
                    if later(i) and half == 1:
                        pe.wait_ge(z2h_made, i * 2)
                    for t in range(HT):
                        mm = nc.tensor.transpose((b7, b6)[half][:, t * P:(t + 1) * P], z[:, half * HT + t, :], ident[:])
                    mm.then_inc(front_mm, 1)
                if kind in ("q", "k"):
                    w = "qk".index(kind)
                    pe.wait_ge(ztl_made, i * 2 + half + 1)
                    pe.wait_ge(zth_made, i * 2 + half + 1)
                    if w == 0 and half and later(i):
                        pe.wait_ge(route_step, (i * 2 - 1) * ROUTE + 1)
                    elif w == 0 and half:
                        pe.wait_ge(v_made, i * 2 + 1)
                    if w and half == 0:
                        pe.wait_ge(qkh_made, i * 4 + 1)
                    split_mm((b6 if half and w else b7)[:], wqk_h[:, w, :], wqk_l[:, w, :], zt_h[:, halfs(half)],
                             zt_l[:, halfs(half)]).then_inc(front_mm, 1)
                if kind == "v":
                    if half:
                        pe.wait_ge(qkh_made, i * 4 + 3)
                    elif later(i):
                        pe.wait_ge(base_made, i * 2 - 1)
                    else:
                        pe.wait_ge(qkh_made, i * 4 + 2)
                    for t in range(HT):
                        mm = nc.tensor.matmul(b7[:, t * P:(t + 1) * P],
                                              zt[:, (half * HT + t) * P:(half * HT + t + 1) * P],
                                              wv_sb[:], start=True, stop=True)
                    mm.then_inc(front_mm, 1)

            def score(i, s):
                u, t, j = SCORE_STEPS[s]
                hd = UNITS[u][0] * G4 + j
                if s == 0:
                    pe.wait_ge(stack_in[0], i * 192 + 192)
                    if later(i):
                        pe.wait_ge(exp_done, i * NP_ * G4)
                if s == UNIT_S:
                    pe.wait_ge(ml_made, i * NU + 1)
                if s == 2 * UNIT_S:
                    pe.wait_ge(stack_in[1], i * 192 + 192)
                    if later(i):
                        pe.wait_ge(sel_made, i * TILES)
                if s >= 2:
                    pe.wait_ge(s_taken, i * NS + s - 1)
                n = (t + 1) * P
                dst = pair[s % 2] if t >= HT else (b4, b5)[s % 2]
                for a, b in ([(0, max(256, n))] if n <= HALF else [(0, HALF), (HALF, max(HALF + 256, n))]):
                    mm = nc.tensor.matmul(dst[:, a:b], q_stack[0:STACK, t // HT, hd, t % HT * P:(t % HT + 1) * P],
                                          k_stack[0:STACK, hd // 2, a:b], start=True, stop=True)
                mm.then_inc(s_ready, 1)

            def turn(i, u):
                if u == 2 and later(i):
                    pe.wait_ge(cnt_taken, i * 2)
                if u == 2:
                    pe.wait_ge(v_made, i * 2 + 2)
                if u == 3:
                    pe.wait_ge(ml_made, i * NU + 3)
                pe.wait_ge(s_taken, i * NS + (u + 1) * UNIT_S)
                nc.tensor.transpose((b4 if u < 2 else b7)[0:UNIT_S, 0:P], mx[:, u * UNIT_S:(u + 1) * UNIT_S],
                                    ident[:]).then_inc(m_turned, 1)

            def prob(i, k, j):
                u, kt = PROB_STEPS[k]
                g, half = UNITS[u]
                q0, c0 = prob_columns(k)
                if kt == 0 and j == 0:
                    pe.wait_ge(m_in[u], i * 32 + 32)
                if k == 0 and j == 0:
                    pe.wait_ge(ml_made, i * NU + 2)
                p = k * G4 + j
                if p >= 2:
                    pe.wait_ge(exp_done, i * NP_ * G4 + p - 1)
                hd = g * G4 + j
                nc.tensor.matmul((b4, b5)[p % 2][:, c0:HALF], k_stack[:, hd // 2, kt * P:(kt + 1) * P],
                                 q_stack[:, half, hd, c0:HALF], start=True, stop=True).then_inc(st_ready, 1)

            def weigh(i, k):
                u, kt = PROB_STEPS[k]
                g, half = UNITS[u]
                q0, _ = prob_columns(k)
                pe.wait_ge(exp_done, i * NP_ * G4 + (k + 1) * G4)
                if k in DIAG:
                    pe.wait_ge(mask_done, i * len(DIAG) + DIAG.index(k) + 1)
                if kt == 0 and u == 0:
                    pe.wait_ge(v_made, i * 2 + 2)
                    pe.wait_ge(qkh_made, i * 4 + 4)
                    if later(i):
                        pe.wait_ge(base_made, i * 2)
                if kt == 0 and u > 0:
                    pe.wait_ge(pv_taken, i * NU + u)
                for j in range(G4):
                    mm = nc.tensor.matmul(b6[32 * j:32 * j + VW, q0:HALF], v[:, kt, g * G4 + j, :],
                                          pt[:, k % PT_SLOTS, j, q0:HALF], start=(kt == 0),
                                          stop=(kt == HT * (half + 1) - 1), tile_position=(0, 32 * j))
                mm.then_inc(pv_done, 1)

            def post(i, st, more):
                kind, half = st[0], st[1]
                if kind == "to":
                    pe.wait_ge(pv_taken, i * NU + 2 * half + 2)
                    if half == 0:
                        pe.wait_ge(s_taken, (i + 1) * NS)
                    elif more:
                        pe.wait_ge(v_made, (i + 1) * 2 + 1)
                    else:
                        pe.wait_ge(base_made, i * 2 + 1)
                    for n in range(2):
                        for m in range(2):
                            t = half * HT + 2 * n + m
                            for g in range(2):
                                to = m * 256 + g * P
                                dst = (b6, b7)[n][:, to:to + P] if half else pair[0][:, n * HALF + to:n * HALF + to + P]
                                mm = nc.tensor.transpose(dst, ot[:, g, t * P:(t + 1) * P], ident[:])
                        mm.then_inc(to_ready, 1)
                if kind == "ant":
                    pe.wait_ge(an_made, i * HT + 2 * half + 2)
                    for t in range(HT):
                        mm = nc.tensor.transpose((b6 if half else pair[1])[:, t * P:(t + 1) * P],
                                                 an[:, half * HT + t, :], ident[:])
                    mm.then_inc(ant_ready, 1)
                if kind == "oproj":
                    pe.wait_ge(ant_made, i * 2 + half + 1)
                    for t in range(HT):
                        tt = half * HT + t
                        dst = b7[:, t * P:(t + 1) * P] if half else pair[1][:, HALF + t * P:HALF + (t + 1) * P]
                        mm = nc.tensor.matmul(dst, ant[:, tt * P:(tt + 1) * P], wo_sb[:], start=True, stop=True)
                    mm.then_inc(o_ready, 1)
                if kind == "z2t":
                    pe.wait_ge(z2_made, i * TILES + (half + 1) * HT)
                    if half and more:
                        pe.wait_ge(h_made, (i + 1) * 2 + 2)
                    for t in range(HT):
                        mm = nc.tensor.transpose((b6 if half else pair[0])[:, t * P:(t + 1) * P],
                                                 z2[:, half * HT + t, :], ident[:])
                    mm.then_inc(z2t_ready, 1)
                if kind == "gates":
                    pe.wait_ge(z2t_made, i * 2 + half + 1)
                    for t in range(HT):
                        tt = half * HT + t
                        to = (0 if half else HALF) + t * GATE_W
                        mm = nc.tensor.matmul((b7 if half else pair[0])[:, to:to + GATE_W],
                                              z2t[:, tt * P:(tt + 1) * P], wgate_sb[:], start=True, stop=True)
                    mm.then_inc(gl_ready, 1)

            def forward(i, st, more):
                kind = st[0]
                if kind == "in":
                    q, ab = st[1:]
                    ex, c, half = IN_STEPS[q]
                    ab_pair = pair[q % 2]
                    if q % 4 == 0 and ab == 0:
                        pe.wait_ge(z2h_made, i * 2 + half + 1)
                        pe.wait_ge(z2l_made, i * 2 + half + 1)
                    if ab:
                        pass
                    elif q == 0:
                        pe.wait_ge(route_step, i * 2 * ROUTE + 1)
                    elif q == 1:
                        pe.wait_ge(h2_made, i * 2 + 1)
                    elif q % 4 < 2:
                        pe.wait_ge(sel_made, i * TILES + q - 1)
                    else:
                        pe.wait_ge(hid_made, i * NIN + q - 1)
                    w0 = ex * 2 * HID + ab * HID + c * P
                    mm = split_mm(ab_pair[:, ab * HALF:(ab + 1) * HALF], win_h[:, w0:w0 + P],
                                  win_l[:, w0:w0 + P], z2t_h[:, halfs(half)], z2t_l[:, halfs(half)])
                    mm.then_inc(in_ready, 1)
                elif kind == "counts":
                    half = st[1]
                    pe.wait_ge(route_step, (i * 2 + half + 1) * ROUTE)
                    if half == 0 and more:
                        pe.wait_ge(qkh_made, (i + 1) * 4 + 2)
                    elif half == 0:
                        pe.wait_ge(ml_made, (i + 1) * NU)
                    elif more:
                        pe.wait_ge(v_made, (i + 1) * 2 + 2)
                    for t in range(HT):
                        mm = nc.tensor.transpose(b7[0:EXPERTS + 1, t * P:(t + 1) * P], cnt[:, half * HT + t, :], ident[:])
                    mm.then_inc(cnt_ready, 1)
                elif kind == "shared":
                    half = st[1]
                    pe.wait_ge(hid_made, i * NIN + (half + 1) * 4)
                    pe.wait_ge(cnt_taken, i * 2 + half + 1)
                    if half and more:
                        pe.wait_ge(qkh_made, (i + 1) * 4 + 4)
                    elif half:
                        pe.wait_ge(z2h_made, i * 2 + 2)
                    for t in range(HT):
                        dst = (b7, b6)[half][:, t * P:(t + 1) * P]
                        tok = slice(t * P, (t + 1) * P)
                        for c in range(HID // P):
                            nc.tensor.matmul(dst, hid[:, 0, c, tok], wshared_sb[:, c, :], start=(c == 0), stop=False)
                        mm = nc.tensor.matmul(dst, cnt_t[:, tok], wbias_sb[:], start=False, stop=True)
                    mm.then_inc(shared_ready, 1)
                elif kind == "expert":
                    t, g = st[1:]
                    dst_pair = pair[t % 2]
                    if t % HT == 0 and g == 0:
                        pe.wait_ge(hidl_made, i * 4 + (t // HT + 1) * 2)
                        pe.wait_ge(hidh_made, i * 4 + (t // HT + 1) * 2)
                    if g:
                        pass
                    elif t % HT < 2:
                        pe.wait_ge(hid_made, i * NIN + t + 3)
                    else:
                        pe.wait_ge(sel_made, i * TILES + t - 1)
                    tok = slice(t % HT * P, (t % HT + 1) * P)
                    dst = dst_pair[:, g * HALF:(g + 1) * HALF]
                    w = slice(g * HALF, (g + 1) * HALF)
                    for c in range(HID // P):
                        nc.tensor.matmul(dst, hid_h[:, c, tok], wex_h[:, c, w], start=(c == 0), stop=False)
                        nc.tensor.matmul(dst, hid_h[:, c, tok], wex_l[:, c, w], start=False, stop=False)
                        mm = nc.tensor.matmul(dst, hid_l[:, c, tok], wex_h[:, c, w], start=False,
                                              stop=(c == HID // P - 1))
                    mm.then_inc(ex_ready, 1)

            def stage(i, st, more=True):
                if st[0] == "score":
                    score(i, st[1])
                elif st[0] == "turn":
                    turn(i, st[1])
                elif st[0] == "prob":
                    prob(i, st[1], st[2])
                elif st[0] == "weigh":
                    weigh(i, st[1])
                elif of_next_image(st):
                    front(i, st[0], st[1])
                elif st[0] in ("in", "counts", "shared", "expert"):
                    forward(i, st, more)
                elif st[0] != "combine":
                    post(i, st, more)

            def image(i):
                for st in PERIOD:
                    stage(i + of_next_image(st), st)

            pe.wait_ge(w_in0, 2 * 16)
            stage(0, FIRST[0])
            pe.wait_ge(w_in1, 7 * 16)
            pe.wait_ge(ident_made, 1)
            pe.wait_ge(wsplit_qk, 4)
            for st in FIRST[1:]:
                stage(0, st)
            pe.wait_ge(ones_in, HEADS // 2 * 16)
            pe.wait_ge(w_in2, 9 * 16)
            pe.wait_ge(wsplit_h, 2)
            pe.wait_ge(wsplit_l, 2)
            image(0)
            with pe.Fori(1, B - 1) as i:
                image(i)
            for st in LAST:
                stage(B - 1, st, False)

        @block.vector
        def _(dve):
            def front(i, kind, half):
                if kind == "emb":
                    dve.wait_ge(front_mm, front_step(i, "emb", half))
                    nc.vector.tensor_tensor(h[:, tiles(half), :], (b7, b6)[half][:].rearrange("p (t c) -> p t c", c=P),
                                            pos_sb[:, tiles(half), :], ALU.add).then_inc(h_made, 1)
                    dve.wait_ge(h_made, i * 2 + half + 1)
                    for t in range(half * HT, (half + 1) * HT):
                        nc.vector.bn_stats(stats[:, t, :], h[:, t, :]).then_inc(stat1, 1)
                    alone(dve, stat1, i * TILES + (half + 1) * HT)
                    for t in range(half * HT, (half + 1) * HT):
                        nc.vector.bn_aggr(mv[:, t, :], stats[:, t, :]).then_inc(mv_made, 1)
                if kind == "turn1":
                    dve.wait_ge(rs_made, i * 2 + half + 1)
                    for t in range(half * HT, (half + 1) * HT):
                        nc.vector.tensor_scalar(z[:, t, :], h[:, t, :], mv[:, t, 0:1], rs1[:, t:t + 1],
                                                ALU.subtract, ALU.mult).then_inc(z_made, 1)
                if kind == "v":
                    dve.wait_ge(front_mm, front_step(i, "v", half))
                    bias = bv_sb[:].rearrange("p (h d) -> p h d", d=DH).unsqueeze(1)
                    nc.vector.tensor_tensor(v[:, tiles(half), :, 0:DH],
                                            b7[:].rearrange("p (t h d) -> p t h d", h=HEADS, d=DH),
                                            bias.to_broadcast([P, HT, HEADS, DH]), ALU.add).then_inc(v_made, 1)

            def maxima_split(i, u):
                dve.wait_ge(m_turned, i * NU + u + 1)
                src = (b4 if u < 2 else b7)[0:UNIT_S, 0:P]
                nc.vector.tensor_copy(mrow_h[:, u, :], src).then_inc(mh_made, 1)
                dve.wait_ge(mh_made, i * NU + u + 1)
                nc.vector.tensor_tensor(mrow_l[:, u, :], src, mrow_h[:, u, :].bitcast(F32),
                                        ALU.subtract).then_inc(ml_made, 1)

            def score(i, s):
                u, t, j = SCORE_STEPS[s]
                n = (t + 1) * P
                col = u * UNIT_S + j * HT + t % HT
                alone(dve, s_ready, i * NS + s + 1)
                src = (pair[s % 2] if t >= HT else (b4, b5)[s % 2])[:, 0:n]
                nc.vector.tensor_tensor_reduce(src, src, causal[:, S - n:S], 1.0, -3.0e38, ALU.add, ALU.max,
                                               mx[:, col:col + 1]).then_inc(s_taken, 1)

            def post(i, st):
                kind, half = st[0], st[1]
                if kind == "to":
                    for m in range(2):
                        n = 2 * half + m
                        dve.wait_ge(to_ready, i * HT + n + 1)
                        src = ((b6, b7)[m][:] if half else pair[0][:, m * HALF:(m + 1) * HALF]).rearrange(
                            "p (k w) -> p k w", w=VW)
                        rc = rec[:, 2 * n:2 * n + 2, :].rearrange("p t h -> p (t h)")
                        nc.vector.reciprocal(rc, src[:, :, DH]).then_inc(rec_made, 1)
                        dve.wait_ge(rec_made, i * HT + n + 1)
                        nc.vector.tensor_tensor(an[:, 2 * n:2 * n + 2, :].rearrange("p t (h d) -> p (t h) d", d=DH),
                                                src[:, :, 0:DH], rc.unsqueeze(2).to_broadcast([P, 2 * HEADS, DH]),
                                                ALU.mult).then_inc(an_made, 1)
                if kind == "oproj":
                    dve.wait_ge(hb_made, i * 2 + half + 1)
                    if later(i):
                        dve.wait_ge(out_done[half], i * 16)
                    src = b7[:] if half else pair[1][:, HALF:2 * HALF]
                    dve.wait_ge(o_ready, i * 2 + half + 1)
                    nc.vector.tensor_tensor(h2[:, tiles(half), :], src.rearrange("p (t c) -> p t c", c=P),
                                            h[:, tiles(half), :], ALU.add).then_inc(h2_made, 1)
                    dve.wait_ge(h2_made, i * 2 + half + 1)
                    for t in range(half * HT, (half + 1) * HT):
                        nc.vector.bn_stats(stats2[:, t, :], h2[:, t, :]).then_inc(stat2, 1)
                    alone(dve, stat2, i * TILES + (half + 1) * HT)
                    for t in range(half * HT, (half + 1) * HT):
                        nc.vector.bn_aggr(mv2[:, t, :], stats2[:, t, :]).then_inc(mv2_made, 1)
                if kind == "z2t":
                    dve.wait_ge(ln2_step, (i * 2 + half + 1) * LN_STEPS)
                    for t in range(half * HT, (half + 1) * HT):
                        nc.vector.tensor_scalar(z2[:, t, :], h2[:, t, :], mv2[:, t, 0:1], rs2[:, t:t + 1],
                                                ALU.subtract, ALU.mult).then_inc(z2_made, 1)
                if kind == "route":
                    route(i, half, st[2])

            def route(i, half, part):
                base = (i * 2 + half) * ROUTE
                T = tiles(half)

                def needs(n):
                    dve.wait_ge(route_step, base + n)

                def step(ins):
                    ins.then_inc(route_step, 1)

                def over_i(ap):
                    return ap.unsqueeze(2).to_broadcast([P, HT, EG, EG])

                def over_j(ap):
                    return ap.unsqueeze(3).to_broadcast([P, HT, EG, EG])

                def square(ap):
                    return ap[:, T, :].rearrange("p t (i j) -> p t i j", j=EG)

                gmb = gm[:, T, :].unsqueeze(3).to_broadcast([P, HT, GROUPS, EG])
                if part == 0:
                    dve.wait_ge(gl_ready, i * 2 + half + 1)
                    src = (b7[:, 0:HT * GATE_W] if half else pair[0][:, HALF:HALF + HT * GATE_W])
                    step(nc.vector.tensor_tensor(gl[:, T, :], src.rearrange("p (t n) -> p t n", n=GATE_W)[:, :, 0:NGATE],
                                                 bgate_sb[:].unsqueeze(1).to_broadcast([P, HT, NGATE]), ALU.add))
                    needs(1)
                    step(nc.vector.tensor_tensor(gm[:, T, 0:1], gl[:, T, 1:2], gl[:, T, 0:1], ALU.is_le))
                    step(nc.vector.tensor_tensor(gm[:, T, 1:2], gl[:, T, 1:2], gl[:, T, 0:1], ALU.is_gt))
                    needs(3)
                    step(nc.vector.tensor_tensor(both[:, T, :, :], gl[:, T, GROUPS:].rearrange("p t (g e) -> p t g e", e=EG),
                                                 gmb, ALU.mult))
                    needs(4)
                    step(nc.vector.tensor_tensor(esel[:, T, :], both[:, T, 0, :], both[:, T, 1, :], ALU.add))
                    needs(5)
                    step(nc.vector.tensor_reduce(emax[:, T], esel[:, T, :], AX.X, ALU.max))
                    step(nc.vector.tensor_tensor(square(cmp_gt), over_i(esel[:, T, :]), over_j(esel[:, T, :]), ALU.is_gt))
                    step(nc.vector.tensor_tensor(square(cmp_eq), over_i(esel[:, T, :]), over_j(esel[:, T, :]), ALU.is_equal))
                    needs(6)
                    step(nc.vector.tensor_tensor(esub[:, T, :], esel[:, T, :], emax[:, T].unsqueeze(2).to_broadcast(
                        [P, HT, EG]), ALU.subtract))
                if part == 1:
                    needs(9)
                    step(nc.vector.tensor_tensor(cmp_tie[:, T, :], cmp_eq[:, T, :], tri[:].unsqueeze(1).to_broadcast(
                        [P, HT, EG * EG]), ALU.mult))
                    needs(10)
                    step(nc.vector.tensor_tensor(cmp_all[:, T, :], cmp_gt[:, T, :], cmp_tie[:, T, :], ALU.add))
                    needs(11)
                    step(nc.vector.tensor_reduce(rank[:, T, :], square(cmp_all), AX.X, ALU.add))
                    needs(12)
                    step(nc.vector.tensor_scalar(top[:, T, :], rank[:, T, :], 1.5, None, ALU.is_lt))
                    needs(13)
                    step(nc.vector.tensor_tensor(cnt[:, T, 0:EXPERTS].rearrange("p t (g e) -> p t g e", e=EG),
                                                 top[:, T, :].unsqueeze(2).to_broadcast([P, HT, GROUPS, EG]), gmb, ALU.mult))
                if part == 2:
                    needs(14)
                    dve.wait_ge(eexp_done, i * 2 + half + 1)
                    step(nc.vector.tensor_tensor(topp[:, T, :], eprob[:, T, :], top[:, T, :], ALU.mult))
                    step(nc.vector.tensor_reduce(esum[:, T], eprob[:, T, :], AX.X, ALU.add))
                    needs(16)
                    step(nc.vector.tensor_reduce(tsum[:, T], topp[:, T, :], AX.X, ALU.add))
                    needs(17)
                    step(nc.vector.scalar_tensor_tensor(tden[:, T], esum[:, T], 1e-8, tsum[:, T], ALU.mult, ALU.add))
                    needs(18)
                    step(nc.vector.reciprocal(trec[:, T], tden[:, T]))
                    needs(19)
                    step(nc.vector.tensor_tensor(wsel[:, T, :], topp[:, T, :], trec[:, T].unsqueeze(2).to_broadcast(
                        [P, HT, EG]), ALU.mult))

            def forward(i, st):
                kind = st[0]
                if kind == "in":
                    q, second = st[1:]
                    ex, c, half = IN_STEPS[q]
                    if not second:
                        return
                    ab = pair[q % 2]
                    if later(i) or q:
                        dve.wait_ge(hid_made, i * NIN + q)
                    if q % 4 < 2 and (later(i) or half):
                        dve.wait_ge(ex_step, slot_summed(i, q))
                    dve.wait_ge(tanh_done, i * NIN + q + 1)
                    dve.wait_ge(in_ready, (i * NIN + q + 1) * 2)
                    nc.vector.scalar_tensor_tensor(from_dve[:, q % 2, :], from_act[:, q % 2, :], 1.0, ab[:, 0:HALF],
                                                   ALU.add, ALU.mult).then_inc(gate_made, 1)
                    dve.wait_ge(gate_made, i * NIN + q + 1)
                    if ex and (later(i) or half):
                        dve.wait_ge(hidl_made, i * 4 + 2 * half)
                    elif later(i) or half:
                        dve.wait_ge(shared_ready, i * 2 + half)
                    nc.vector.scalar_tensor_tensor(hid[:, ex, c, :], from_dve[:, q % 2, :], 0.5,
                                                   ab[:, HALF:2 * HALF], ALU.mult, ALU.mult).then_inc(hid_made, 1)
                elif kind == "shared":
                    half = st[1]
                    dve.wait_ge(shared_ready, i * 2 + half + 1)
                    nc.vector.tensor_tensor(acc[:, tiles(half), :], (b7, b6)[half][:].rearrange("p (t c) -> p t c", c=P),
                                            h2[:, tiles(half), :], ALU.add).then_inc(base_made, 1)
                elif kind == "expert":
                    t, second = st[1:]
                    slot = t % 2
                    if not second:
                        return
                    if t % HT == 0:
                        dve.wait_ge(hid_made, i * NIN + (t // HT + 1) * 4)
                        dve.wait_ge(route_step, (i * 2 + t // HT + 1) * ROUTE)
                    elif t % HT >= 2:
                        dve.wait_ge(ex_step, (i * TILES + t - 1) * COMBINE)
                    dve.wait_ge(sela_made, i * TILES + t + 1)
                    dve.wait_ge(ex_ready, (i * TILES + t + 1) * GROUPS)
                    nc.vector.scalar_tensor_tensor(from_dve[:, slot, :], pair[slot][:, HALF:2 * HALF], gm[:, t, 1:2],
                                                   from_act[:, slot, :], ALU.mult, ALU.add).then_inc(sel_made, 1)

            def stage(i, st):
                if st[0] == "score":
                    score(i, st[1])
                elif st[0] == "turn":
                    maxima_split(i, st[1])
                elif of_next_image(st):
                    front(i, st[0], st[1])
                elif st[0] == "combine":
                    pass
                elif st[0] in ("in", "counts", "shared", "expert"):
                    forward(i, st)
                else:
                    post(i, st)

            def image(i):
                for st in PERIOD:
                    stage(i + of_next_image(st), st)

            nc.vector.memset(words(k_stack[:, 0:2, :]), 0.0).then_inc(stacks_zeroed, 1)
            dve.wait_ge(w_in0, 2 * 16)
            stage(0, FIRST[0])
            dve.wait_ge(w_in1, 7 * 16)
            for n, w in enumerate((wq_sb, wk_sb)):
                nc.vector.tensor_copy(wqk_h[:, n, :], w[:]).then_inc(wsplit_qk, 1)
            dve.wait_ge(wsplit_qk, 2)
            for n, w in enumerate((wq_sb, wk_sb)):
                nc.vector.tensor_tensor(wqk_l[:, n, :], w[:], wqk_h[:, n, :].bitcast(F32),
                                        ALU.subtract).then_inc(wsplit_qk, 1)
            stage(0, FIRST[1])
            nc.vector.memset(words(k_stack[:, 2:, :]), 0.0).then_inc(stacks_zeroed, 1)
            dve.wait_ge(const_made, CONSTS)
            for st in FIRST[2:]:
                stage(0, st)
            dve.wait_ge(w_in2, 9 * 16)
            image(0)
            with dve.Fori(1, B - 1) as i:
                image(i)
            for st in LAST:
                stage(B - 1, st)

        @block.scalar
        def _(act):
            def front(i, kind, half):
                if kind == "turn1":
                    if later(i):
                        act.wait_ge(z2l_made, i * 2 - 1 + half)
                    act.wait_ge(front_mm, front_step(i, "turn1", half))
                    src = (b7, b6)[half]
                    nc.scalar.copy(zt[:, halfs(half)], src[:]).then_inc(zt_made, 1)
                    nc.scalar.copy(zt_h[:, halfs(half)], src[:]).then_inc(zth_made, 1)
                if kind in ("q", "k"):
                    w = "qk".index(kind)
                    src, bias = (b6 if half and w else b7), (bq_sb, bk_sb)[w]
                    act.wait_ge(front_mm, front_step(i, kind, half))
                    nc.scalar.activation(qk[:, w, halfs(half)], src[:], ACT.Identity,
                                         bias=bias[:, 0:1]).then_inc(qk_made, 1)
                    nc.scalar.activation(qk_h[:, w, halfs(half)], src[:], ACT.Identity,
                                         bias=bias[:, 0:1]).then_inc(qkh_made, 1)

            def take(i, u):
                g, half = UNITS[u]
                act.wait_ge(pv_done, i * NP_ + UNIT_LAST[u] + 1)
                nc.scalar.copy(ot[:, g, halfs(half)], b6[:]).then_inc(pv_taken, 1)

            def prob(i, k, j):
                u, kt = PROB_STEPS[k]
                q0, _ = prob_columns(k)
                if j == 0 and (k >= PT_SLOTS or later(i)):
                    act.wait_ge(pv_done, i * NP_ + max(0, k - PT_SLOTS + 1))
                p = k * G4 + j
                act.wait_ge(st_ready, i * NP_ * G4 + p + 1)
                nc.scalar.activation(pt[:, k % PT_SLOTS, j, q0:HALF], (b4, b5)[p % 2][:, q0:HALF], ACT.Exp,
                                     scale=0.25).then_inc(exp_done, 1)

            def post(i, st):
                kind, half = st[0], st[1]
                if kind == "ant":
                    act.wait_ge(ant_ready, i * 2 + half + 1)
                    nc.scalar.copy(ant[:, halfs(half)], b6[:] if half else pair[1][:, 0:HALF]).then_inc(ant_made, 1)
                if kind == "z2t":
                    src = b6[:] if half else pair[0][:, 0:HALF]
                    act.wait_ge(z2t_ready, i * 2 + half + 1)
                    for dst, made in ((z2t, z2t_made), (z2t_h, z2h_made)):
                        nc.scalar.activation(dst[:, halfs(half)], src, ACT.Identity, bias=lnb_sb[:, 0:1],
                                             scale=lns_sb[:, 0:1]).then_inc(made, 1)
                if kind == "route" and st[2] == 0:
                    act.wait_ge(route_step, (i * 2 + half) * ROUTE + 9)
                    nc.scalar.activation(eprob[:, tiles(half), :], esub[:, tiles(half), :], ACT.Exp).then_inc(eexp_done, 1)

            def forward(i, st):
                kind = st[0]
                if kind == "in":
                    q, second = st[1:]
                    half = IN_STEPS[q][2]
                    if not second:
                        if q % 4 < 2 and (later(i) or half):
                            act.wait_ge(ex_step, slot_summed(i, q))
                        act.wait_ge(in_ready, (i * NIN + q) * 2 + 1)
                        nc.scalar.activation(from_act[:, q % 2, :], pair[q % 2][:, 0:HALF], ACT.Tanh,
                                             scale=0.5).then_inc(tanh_done, 1)
                        return
                    if IN_STEPS[q - 1][0] == 1 and q % 4:
                        _, c, half = IN_STEPS[q - 1]
                        act.wait_ge(hid_made, i * NIN + q)
                        if later(i) or half:
                            act.wait_ge(ex_ready, (i * TILES + half * HT) * GROUPS)
                        nc.scalar.copy(hid_h[:, c, :], hid[:, 1, c, :]).then_inc(hidh_made, 1)
                elif kind == "expert":
                    t, second = st[1:]
                    slot = t % 2
                    if second:
                        return
                    if t % HT >= 2:
                        act.wait_ge(ex_step, (i * TILES + t - 1) * COMBINE)
                    act.wait_ge(ex_ready, (i * TILES + t) * GROUPS + 1)
                    if t % HT == 0:
                        act.wait_ge(route_step, (i * 2 + t // HT + 1) * ROUTE)
                    nc.scalar.mul(from_act[:, slot, :], pair[slot][:, 0:HALF], gm[:, t, 0:1]).then_inc(sela_made, 1)
                elif kind == "combine":
                    t = st[1]
                    act.wait_ge(sel_made, i * TILES + t + 1)
                    for e in range(EG):
                        part = slice(e * P, (e + 1) * P)
                        nc.scalar.mul(from_act[:, t % 2, part], from_dve[:, t % 2, part],
                                      wsel[:, t, e:e + 1]).then_inc(weighted, 1)
                elif kind == "counts":
                    half = st[1]
                    act.wait_ge(cnt_ready, i * 2 + half + 1)
                    if later(i) or half:
                        act.wait_ge(base_made, i * 2 + half)
                    nc.scalar.copy(cnt_t[:], b7[0:EXPERTS + 1, :]).then_inc(cnt_taken, 1)

            def stage(i, st):
                if st[0] == "prob":
                    prob(i, st[1], st[2])
                elif st[0] == "take":
                    take(i, st[1])
                elif st[0] in ("turn1", "q", "k"):
                    front(i, st[0], st[1])
                elif st[0] in ("in", "counts", "expert", "combine"):
                    forward(i, st)
                elif st[0] in ("ant", "z2t", "route"):
                    post(i, st)

            def image(i):
                for st in PERIOD:
                    stage(i + of_next_image(st), st)

            act.wait_ge(w_in1, 7 * 16)
            for st in FIRST:
                stage(0, st)
            act.wait_ge(w_in2, 9 * 16)
            nc.scalar.copy(win_h[:], win_sb).then_inc(wsplit_h, 1)
            nc.scalar.copy(wex_h[:], wex_sb).then_inc(wsplit_h, 1)
            image(0)
            with act.Fori(1, B - 1) as i:
                image(i)
            for st in LAST:
                stage(B - 1, st)

        @block.gpsimd
        def _(pool):
            nc.gpsimd.memset(half_pow[:], -0.5).then_inc(const_made, 1)
            nc.gpsimd.memset(ident[:], 0.0).then_inc(zeroed, 1)
            pool.wait_ge(zeroed, 1)
            nc.gpsimd.affine_select(out=ident[:], in_=ident[:], compare_op=ALU.not_equal, fill=1.0, base=0,
                                    pattern=[[-1, P]], channel_multiplier=1).then_inc(ident_made, 1)
            nc.gpsimd.memset(words(q_stack[:]), 0.0).then_inc(stacks_zeroed, 1)
            pool.wait_ge(const_made, 1)

            def constants():
                nc.gpsimd.memset(causal[:], 0.0).then_inc(zeroed, 1)
                nc.gpsimd.memset(tri[:], 1.0).then_inc(zeroed, 1)
                nc.gpsimd.memset(v[:], 0.0).then_inc(zeroed, 1)
                pool.wait_ge(zeroed, 4)
                nc.gpsimd.affine_select(out=causal[:, S - P:S], in_=causal[:, S - P:S], compare_op=ALU.is_ge,
                                        fill=MASK, base=0, pattern=[[-1, P]],
                                        channel_multiplier=1).then_inc(const_made, 1)
                nc.gpsimd.affine_select(out=tri[:].rearrange("p (i j) -> p i j", j=EG),
                                        in_=tri[:].rearrange("p (i j) -> p i j", j=EG), compare_op=ALU.is_gt,
                                        fill=0.0, base=0, pattern=[[1, EG], [-1, EG]],
                                        channel_multiplier=0).then_inc(const_made, 1)
                nc.gpsimd.memset(v[:, :, :, DH:DH + 1], 1.0).then_inc(const_made, 1)
                nc.gpsimd.memset(words(minus1), -1.0).then_inc(const_made, 1)
                nc.gpsimd.memset(cnt[:, :, EXPERTS:EXPERTS + 1], 1.0).then_inc(const_made, 1)

            def front(i, kind, half):
                if kind == "emb":
                    alone(pool, mv_made, i * TILES + (half + 1) * HT)
                    nc.gpsimd.tensor_scalar(var1[:, tiles(half)], mv[:, tiles(half), 1], EPS, None,
                                            ALU.add).then_inc(var_made, 1)
                    pool.wait_ge(var_made, i * 2 + half + 1)
                    nc.gpsimd.tensor_tensor(rs1[:, tiles(half)], var1[:, tiles(half)], half_pow[:, tiles(half)],
                                            ALU.pow).then_inc(rs_made, 1)
                if kind == "turn1":
                    pool.wait_ge(zth_made, i * 2 + half + 1)
                    nc.gpsimd.tensor_tensor(zt_l[:, halfs(half)], zt[:, halfs(half)], zt_h[:, halfs(half)].bitcast(F32),
                                            ALU.subtract).then_inc(ztl_made, 1)
                if kind in ("q", "k"):
                    w = "qk".index(kind)
                    pool.wait_ge(qkh_made, i * 4 + 2 * half + w + 1)
                    nc.gpsimd.tensor_tensor(qk_l[:, w, halfs(half)], qk[:, w, halfs(half)],
                                            qk_h[:, w, halfs(half)].bitcast(F32), ALU.subtract).then_inc(qkl_made, 1)
                if kind == "v":
                    pool.wait_ge(z_made, i * TILES + (half + 1) * HT)
                    nc.gpsimd.tensor_tensor(h[:, tiles(half), :], h[:, tiles(half), :],
                                            bo_sb[:].unsqueeze(1).to_broadcast([P, HT, P]), ALU.add).then_inc(hb_made, 1)

            def mask(i, k):
                q0, _ = prob_columns(k)
                alone(pool, exp_done, i * NP_ * G4 + (k + 1) * G4)
                d = pt[:, k % PT_SLOTS, :, q0:q0 + P]
                nc.gpsimd.affine_select(out=d, in_=d, compare_op=ALU.is_ge, fill=0.0, base=0,
                                        pattern=[[0, G4], [1, P]], channel_multiplier=-1).then_inc(mask_done, 1)

            def post(i, st):
                kind, half = st[0], st[1]
                T = tiles(half)
                if kind == "oproj":
                    alone(pool, mv2_made, i * TILES + (half + 1) * HT)
                    nc.gpsimd.tensor_scalar(var2[:, T], mv2[:, T, 1], 1.0 + EPS, EPS * EPS, ALU.mult,
                                            ALU.add).then_inc(ln2_step, 1)
                    pool.wait_ge(ln2_step, (i * 2 + half) * LN_STEPS + 1)
                    nc.gpsimd.tensor_tensor(rs2[:, T], var2[:, T], half_pow[:, T], ALU.pow).then_inc(ln2_step, 1)
                if kind == "z2t":
                    pool.wait_ge(z2h_made, i * 2 + half + 1)
                    nc.gpsimd.tensor_tensor(z2t_l[:, halfs(half)], z2t[:, halfs(half)],
                                            words(z2t_h[:, halfs(half)]), ALU.subtract).then_inc(z2l_made, 1)

            def split_hidden(i, q):
                ex, c, half = IN_STEPS[q - 1]
                if ex and q % 4:
                    pool.wait_ge(hidh_made, i * 4 + 2 * half + c + 1)
                    nc.gpsimd.tensor_tensor(hid_l[:, c, :], hid[:, 1, c, :], words(hid_h[:, c, :]),
                                            ALU.subtract).then_inc(hidl_made, 1)

            def combine(i, t):
                slot, done = t % 2, (i * TILES + t) * COMBINE
                four, two = from_act[:, slot, :], from_dve[:, slot, 0:2 * P]
                pool.wait_ge(weighted, (i * TILES + t + 1) * EG)
                nc.gpsimd.tensor_tensor(two, four[:, 0:2 * P], four[:, 2 * P:4 * P], ALU.add).then_inc(ex_step, 1)
                if t % HT == 0:
                    pool.wait_ge(base_made, i * 2 + t // HT + 1)
                pool.wait_ge(ex_step, done + 1)
                nc.gpsimd.tensor_tensor(acc[:, t, :], acc[:, t, :], two[:, 0:P], ALU.add).then_inc(ex_step, 1)
                pool.wait_ge(ex_step, done + 2)
                nc.gpsimd.tensor_tensor(acc[:, t, :], acc[:, t, :], two[:, P:2 * P], ALU.add).then_inc(ex_step, 1)

            def stage(i, st):
                if st[0] == "prob":
                    if st[1] in DIAG and st[2] == G4 - 1:
                        mask(i, st[1])
                elif st[0] == "combine":
                    combine(i, st[1])
                elif st[0] in ("emb", "turn1", "q", "k", "v"):
                    front(i, st[0], st[1])
                elif st[0] == "in" and st[2]:
                    split_hidden(i, st[1])
                elif st[0] in ("oproj", "z2t"):
                    post(i, st)

            def image(i):
                for st in PERIOD:
                    stage(i + of_next_image(st), st)

            stage(0, FIRST[0])
            constants()
            pool.wait_ge(w_in1, 7 * 16)
            for st in FIRST[1:]:
                stage(0, st)
            pool.wait_ge(wsplit_h, 1)
            nc.gpsimd.tensor_tensor(win_l[:], win_sb, win_h[:].bitcast(F32), ALU.subtract).then_inc(wsplit_l, 1)
            pool.wait_ge(wsplit_h, 2)
            nc.gpsimd.tensor_tensor(wex_l[:], wex_sb, wex_h[:].bitcast(F32), ALU.subtract).then_inc(wsplit_l, 1)
            image(0)
            with pool.Fori(1, B - 1) as i:
                image(i)
            for st in LAST:
                stage(B - 1, st)


def position_table():
    import math
    position = np.arange(2 * S, dtype=np.float32)[:, None]
    div_term = np.exp(np.arange(0, P, 2, dtype=np.float32) * (-math.log(10000.0) / P))
    pe = np.zeros((2 * S, P), dtype=np.float32)
    pe[:, 0::2] = np.sin(position * div_term)
    pe[:, 1::2] = np.cos(position * div_term)
    return np.ascontiguousarray(pe[:S].reshape(TILES, P, P).transpose(1, 0, 2))


def kernel(**inputs):
    import numpy as _np
    import concourse.bacc as _bacc
    from concourse import mybir as _mybir
    from concourse.bass_utils import run_bass_kernel_spmd as _run

    a = {k: _np.asarray(w) for k, w in inputs.items()}

    def rows(w):
        return _np.broadcast_to(w[None, :], (P, w.shape[0]))

    def column(w):
        return w.reshape(P, 1)

    def by_pairs(w):
        w = w.reshape(-1, HEADS // 2, 2, DH)
        return w.transpose(0, 2, 3, 1).reshape(-1, P)

    laid = {
        "x_t": a["x"].reshape(B * S, F).T,
        "tok_w": a["L0_tok_W"],
        "pos": position_table(),
        "wq": by_pairs(a["L0_attn_Wq"]), "wk": by_pairs(a["L0_attn_Wk"]), "wv": a["L0_attn_Wv"], "wo": a["L0_attn_Wo"],
        "bq": column(by_pairs(a["L0_attn_bq"])), "bk": column(by_pairs(a["L0_attn_bk"])),
        "bv": rows(a["L0_attn_bv"]), "bo": rows(a["L0_attn_bo"]),
        "ln_s": column(a["L0_ffn_ln_scale"]), "ln_b": column(a["L0_ffn_ln_bias"]),
        "w_in": _np.concatenate([a["L0_ffn_shared_in_w"], a["L0_ffn_expert_in_w"]], 0).T,
        "w_shared": a["L0_ffn_shared_out_w"].T.reshape(HID // P, P, P).transpose(1, 0, 2),
        "w_expert": a["L0_ffn_expert_out_weight"].transpose(2, 0, 1).reshape(HID // P, P, EXPERTS * P).transpose(1, 0, 2),
        "w_bias": _np.concatenate([a["L0_ffn_expert_out_bias"], a["L0_ffn_shared_out_b"][None, :]], 0),
        "w_gate": _np.concatenate([a["L0_ffn_group_gate_w"], a["L0_ffn_expert_gate_w"],
                                   _np.zeros((GATE_W - NGATE, P), _np.float32)], 0).T,
        "b_gate": rows(_np.concatenate([a["L0_ffn_group_bias"], a["L0_ffn_expert_bias"]])),
    }
    nc = _bacc.Bacc("TRN2", target_bir_lowering=False, num_devices=1)
    arrays, args = {}, []
    for name, w in laid.items():
        w = _np.ascontiguousarray(w)
        arrays[name] = w
        args.append(nc.dram_tensor(name, w.shape, _mybir.dt.from_np(w.dtype), kind="ExternalInput").ap())
    args.append(nc.dram_tensor("out", (B, S, P), _mybir.dt.float32, kind="ExternalOutput").ap())
    build(nc, *args)
    r = _run(nc, [arrays], core_ids=[0])
    return r.results[0]["out"]
```
